# Optimizing a Trainium2 kernel written in Bass

```python
import numpy as np
import jax
import jax.numpy as jnp

def _softmax(x, axis=-1):
    return jax.nn.softmax(x, axis=axis)

def _gelu(x):
    return jax.nn.gelu(x, approximate=True)

def _silu(x):
    return jax.nn.silu(x)

def _sigmoid(x):
    return jax.nn.sigmoid(x)

def _layernorm(x, axis=-1, eps=1e-05):
    m = jnp.mean(x, axis=axis, keepdims=True)
    v = jnp.var(x, axis=axis, keepdims=True)
    return (x - m) / jnp.sqrt(v + eps)

def _scatter_add(tgt, idx, src, axis=0):
    return tgt.at[idx].add(src)

def _segment_sum(src, seg, n):
    return jax.ops.segment_sum(src, seg, n)
kernel_name = 'mk_gnn_ffn_d1_gnn_r8_54e299'

def setup_inputs(seed: int=0):
    np.random.seed(seed)
    _w = jnp.asarray

    def _rec_inputs():
        import jax
        import jax.numpy as jnp
        _gk = jax.random.key(seed)
        x = -0.0003019 + 1 * jax.random.normal(jax.random.fold_in(_gk, 1), (1250, 1024), jnp.float32)
        src = jax.random.randint(jax.random.fold_in(_gk, 2), (40000,), 0, 1250, jnp.int32)
        dst = jnp.minimum((1250 * jax.random.uniform(jax.random.fold_in(_gk, 3), (40000,)) ** 2.0).astype(jnp.int32), 9999)
        _o = jnp.argsort(dst, stable=True)
        src = src[_o]
        dst = dst[_o]
        return (x, src, dst)
    x, src, dst = _rec_inputs()

    def _L0_gnn_setup():
        import jax, jax.numpy as jnp
        import numpy as np
        N = 2500
        E = 40000
        IN = 1024
        HID = 256
        H = 4
        D = HID // H
        OUT = 1024
        EPS = 1e-06
        NEG_SLOPE = 0.2
        key = jax.random.key(seed)
        ks = jax.random.split(key, 8)
        x = jax.random.normal(ks[0], (N, IN), dtype=jnp.float32)
        edge_index = jax.random.randint(ks[1], (2, E), 0, N, dtype=jnp.int64)
        s = 0.02
        return {'x': x, 'edge_index': edge_index, 'rms_w': jnp.ones((IN,), dtype=jnp.float32), 'W_down': jax.random.normal(ks[2], (IN, HID), dtype=jnp.float32) * s, 'Wl': jax.random.normal(ks[3], (HID, HID), dtype=jnp.float32) * s, 'Wr': jax.random.normal(ks[4], (HID, HID), dtype=jnp.float32) * s, 'att': jax.random.normal(ks[5], (H, D), dtype=jnp.float32) * s, 'W_up': jax.random.normal(ks[6], (HID, OUT), dtype=jnp.float32) * s}
    _L0_gnn_all = _L0_gnn_setup()
    _L0_gnn_in = {k: v for k, v in _L0_gnn_all.items() if k in ('rms_w', 'W_down', 'Wl', 'Wr', 'att', 'W_up')}
    del _L0_gnn_all

    def _L0_ffn_setup():
        import jax, jax.numpy as jnp
        import numpy as np
        HID = 1024
        INTER = 512
        RDIM = 128
        HEADS = 4
        NUM_EXPERTS = 2048
        NUM_KEYS = 128
        TOPK = 8
        B, T = (2, 256)
        key = jax.random.key(seed)
        ks = jax.random.split(key, 8)
        s = lambda fan_in: 1.0 / np.sqrt(fan_in)
        return {'hidden_states': jax.random.normal(ks[0], (B, T, HID), jnp.float32), 'Wq': jax.random.normal(ks[1], (HEADS * RDIM, HID), jnp.float32) * s(HID), 'keys': jax.random.normal(ks[2], (HEADS, NUM_KEYS, 2, RDIM // 2), jnp.float32) * s(RDIM // 2), 'down_embed': jax.random.normal(ks[3], (NUM_EXPERTS, HID), jnp.float32) * 0.02, 'up_embed': jax.random.normal(ks[4], (NUM_EXPERTS, HID), jnp.float32) * 0.02, 'Wg': jax.random.normal(ks[5], (INTER, HID), jnp.float32) * s(HID), 'Wu': jax.random.normal(ks[6], (INTER, HID), jnp.float32) * s(HID), 'Wd': jax.random.normal(ks[7], (HID, INTER), jnp.float32) * s(INTER)}
    _L0_ffn_all = _L0_ffn_setup()
    _L0_ffn_in = {k: v for k, v in _L0_ffn_all.items() if k in ('Wq', 'keys', 'down_embed', 'up_embed', 'Wg', 'Wu', 'Wd')}
    del _L0_ffn_all
    return {'x': x, 'src': src, 'dst': dst, 'L0_gnn_rms_w': _L0_gnn_in['rms_w'], 'L0_gnn_W_down': _L0_gnn_in['W_down'], 'L0_gnn_Wl': _L0_gnn_in['Wl'], 'L0_gnn_Wr': _L0_gnn_in['Wr'], 'L0_gnn_att': _L0_gnn_in['att'], 'L0_gnn_W_up': _L0_gnn_in['W_up'], 'L0_ffn_Wq': _L0_ffn_in['Wq'], 'L0_ffn_keys': _L0_ffn_in['keys'], 'L0_ffn_down_embed': _L0_ffn_in['down_embed'], 'L0_ffn_up_embed': _L0_ffn_in['up_embed'], 'L0_ffn_Wg': _L0_ffn_in['Wg'], 'L0_ffn_Wu': _L0_ffn_in['Wu'], 'L0_ffn_Wd': _L0_ffn_in['Wd']}

def reference(x, src, dst, L0_gnn_rms_w, L0_gnn_W_down, L0_gnn_Wl, L0_gnn_Wr, L0_gnn_att, L0_gnn_W_up, L0_ffn_Wq, L0_ffn_keys, L0_ffn_down_embed, L0_ffn_up_embed, L0_ffn_Wg, L0_ffn_Wu, L0_ffn_Wd):
    import jax
    import jax.numpy as jnp

    def _L0_gnn_ref(x, edge_index, rms_w, W_down, Wl, Wr, att, W_up):
        import jax, jax.numpy as jnp
        import numpy as np
        N = 2500
        E = 40000
        IN = 1024
        HID = 256
        H = 4
        D = HID // H
        OUT = 1024
        EPS = 1e-06
        NEG_SLOPE = 0.2
        n = x.shape[0]
        ms = jnp.mean(jnp.square(x), axis=-1, keepdims=True)
        x = x * jax.lax.rsqrt(ms + EPS) * rms_w
        x = x @ W_down
        loop = jnp.arange(n, dtype=edge_index.dtype)
        src = jnp.concatenate([edge_index[0], loop])
        dst = jnp.concatenate([edge_index[1], loop])
        xl = (x @ Wl).reshape(n, H, D)
        xr = (x @ Wr).reshape(n, H, D)
        msg = xl[src] + xr[dst]
        act = jnp.where(msg > 0, msg, NEG_SLOPE * msg)
        e = jnp.einsum('ehd,hd->eh', act, att)
        m = jax.ops.segment_max(e, dst, num_segments=n)
        p = jnp.exp(e - m[dst])
        denom = jax.ops.segment_sum(p, dst, num_segments=n)
        alpha = p / (denom[dst] + 1e-16)
        out = jax.ops.segment_sum(alpha[..., None] * xl[src], dst, num_segments=n)
        out = out.reshape(n, HID)
        return out @ W_up

    def _L0_ffn_ref(hidden_states, Wq, keys, down_embed, up_embed, Wg, Wu, Wd):
        import jax, jax.numpy as jnp
        import numpy as np
        HID = 1024
        INTER = 512
        RDIM = 128
        HEADS = 4
        NUM_EXPERTS = 2048
        NUM_KEYS = 128
        TOPK = 8
        B, T = (2, 256)
        b, t, _ = hidden_states.shape
        q = hidden_states @ Wq.T
        q = q.reshape(b, t, 2, HEADS, RDIM // 2)
        q = jnp.transpose(q, (2, 0, 1, 3, 4))
        sim = jnp.einsum('pbthn,hkpn->pbthk', q, keys)
        sx, ix = jax.lax.top_k(sim[0], TOPK)
        sy, iy = jax.lax.top_k(sim[1], TOPK)
        all_scores = (sx[..., :, None] + sy[..., None, :]).reshape(b, t, HEADS, TOPK * TOPK)
        all_indices = (ix[..., :, None] * NUM_KEYS + iy[..., None, :]).reshape(b, t, HEADS, TOPK * TOPK)
        scores, pk = jax.lax.top_k(all_scores, TOPK)
        indices = jnp.take_along_axis(all_indices, pk, axis=-1)
        down = down_embed[indices]
        up = up_embed[indices]
        w = jnp.einsum('btd,bthkd->bthk', hidden_states, down)
        w = jax.nn.silu(w) * jax.nn.softmax(scores, axis=-1)
        experts_states = jnp.einsum('bthk,bthkd->btd', w, up)
        mlp = jax.nn.silu(hidden_states @ Wg.T) * (hidden_states @ Wu.T) @ Wd.T
        return mlp + experts_states
    edge_index = jnp.stack([src, dst])
    x = x + _L0_gnn_ref(_layernorm(x, axis=-1), edge_index, L0_gnn_rms_w, L0_gnn_W_down, L0_gnn_Wl, L0_gnn_Wr, L0_gnn_att, L0_gnn_W_up)
    x = x + _L0_ffn_ref(_layernorm(x, axis=-1)[None], L0_ffn_Wq, L0_ffn_keys, L0_ffn_down_embed, L0_ffn_up_embed, L0_ffn_Wg, L0_ffn_Wu, L0_ffn_Wd)[0]
    return x

_drawn_inputs = setup_inputs


def setup_inputs(seed=0):
    import zlib

    import numpy as np

    out = dict(_drawn_inputs(seed))
    spreads = {'L0_gnn_rms_w': (1.0, 0.6)}
    factors = {'L0_gnn_W_down': 3.016,
     'L0_gnn_Wl': 3.027,
     'L0_gnn_Wr': 8.0,
     'L0_gnn_att': 8.0,
     'L0_gnn_W_up': 3.271,
     'L0_ffn_Wq': 8.0,
     'L0_ffn_keys': 8.0,
     'L0_ffn_down_embed': 2.744,
     'L0_ffn_up_embed': 2.717}
    for name, (base, spread) in spreads.items():
        noise = np.random.default_rng([zlib.crc32(name.encode()), seed]).standard_normal(out[name].shape)
        drawn = base * np.exp(spread * noise) if base else spread * noise
        out[name] = jnp.asarray(drawn.astype(out[name].dtype))
    for name, factor in factors.items():
        out[name] = (out[name] * factor).astype(out[name].dtype)
    return out
```

```python
from contextlib import ExitStack

import concourse.bass as bass
from concourse import mybir

F32 = mybir.dt.float32
BF16 = mybir.dt.bfloat16
I32 = mybir.dt.int32
U32 = mybir.dt.uint32
ALU = mybir.AluOpType
ACT = mybir.ActivationFunctionType
AX = mybir.AxisListType
P = 128
BIG = 3.0e38


def gnn_then_peer_ffn(nc, x, src, dst, rms_w, w_down, w_l, w_r, att, w_up, wq_t, keys_t, down_t, up, wg_t, wu_t,
                      wd_t, out):
    N, D = x.shape
    HID = w_down.shape[1]
    HEADS, HD = att.shape
    NT = -(-N // P)
    LAST = N - (NT - 1) * P
    KD = D // P
    KH = HID // P
    T = 8
    HT = T // 2
    CH = T * P
    NCH = src.shape[0] // CH
    MAXV = NT * NCH + 2
    SLOT = HD + 1
    SUMS = HEADS * SLOT
    NG = NT // 2
    GT = 2 * P
    QH = wq_t.shape[1] // (2 * HEADS)
    NK = keys_t.shape[3]
    TOP = 8
    INTER = wg_t.shape[1]
    KI = INTER // P
    NE = up.shape[0]
    NX = NE // NK
    QE = 4
    EB = NE // P // QE
    KEYP = 2 * HEADS
    assert KD * P == D and NG * 2 == NT and HEADS * HD == HID and NK == P and QH * 2 == P

    with ExitStack() as ctx:
        def sb(name, shape, dt=F32):
            return ctx.enter_context(nc.sbuf_tensor(name, shape, dt))

        def sem(name):
            return ctx.enter_context(nc.semaphore(name))

        xs = sb("xs", [P, NT, D])
        acc_all = sb("acc_all", [P, NT + 1, HEADS, SLOT])
        wup_s = sb("wup_s", [P, KH, D])
        ident = sb("ident", [P, P])
        ident_b = sb("ident_b", [P, P], BF16)
        iota_row = sb("iota_row", [P, P])
        iota_part = sb("iota_part", [P, 1])
        win_base = sb("win_base", [P, NT + 1])
        win_node = sb("win_node", [P, NT + 1])
        stats = sb("stats", [P, NT, 2, 6])
        meanvar = sb("meanvar", [P, NT, 2])
        nrm = sb("nrm", [P, 4, NT])
        pace_act = sb("pace_act", [P, 1])
        pace_dve = sb("pace_dve", [P, 1])
        pace_pool = sb("pace_pool", [P, 4], I32)
        zero_pool = sb("zero_pool", [P, 1], I32)
        WS = KD * INTER
        slot = [sb("slot0", [P, WS]), sb("slot1", [P, WS])]
        keys_s = sb("keys_s", [P, HEADS, 2, NK])
        wq_s = slot[0][:].rearrange("p (k n) -> p k n", k=KD)
        wg_s = slot[1][:].rearrange("p (k n) -> p k n", k=KD)
        AR = 27 * 1024
        arena = sb("arena", [P, AR])
        at = [0]

        def carve(n, dt=F32):
            w = n if dt != BF16 else n // 2
            v = arena[:, at[0]:at[0] + w]
            at[0] += w
            assert at[0] <= AR, at[0]
            return v if dt == F32 else v.bitcast(dt)

        xr3 = carve((NT + 1) * 3 * HID, BF16).rearrange("p (t s n) -> p t s n", t=NT + 1, s=3)
        att_b = carve(KH * HEADS).rearrange("p (k h) -> p k h", k=KH)
        dcol = carve(NCH * T)
        m_all = carve((NT + 1) * HEADS).rearrange("p (t h) -> p t h", t=NT + 1)
        visits = carve(2 * MAXV, I32).rearrange("p (a v) -> p a v", a=2)
        n_pairs = carve(2, I32)
        g_at = at[0]
        xl = carve(NT * HID).rearrange("p (t n) -> p t n", t=NT)
        xr = carve(NT * HID).rearrange("p (t n) -> p t n", t=NT)
        s_at = at[0]
        wdn_s = carve(KD * HID).rearrange("p (k n) -> p k n", k=KD)
        wlr_s = carve(KH * 2 * HID).rearrange("p (k n) -> p k n", k=KH)
        zt = carve(KH * GT).rearrange("p (k c) -> p k c", k=KH)
        assert at[0] - s_at >= NT * HID
        s_res = arena[:, s_at:s_at + NT * HID].rearrange("p (t n) -> p t n", t=NT)
        rms_s = carve(KD)
        att_s = carve(HID)
        dst_i = carve(NCH * T, I32)
        m_self = carve(NT * HEADS, BF16)
        e_self = carve(NT * HEADS)
        p_self = carve(NT * HEADS)
        bnd_p = carve(2 * NT)
        bnd_t = carve(4)
        bnd_r = carve(5 * NT).rearrange("p (a w) -> p a w", a=5)
        visits_n = carve(MAXV)
        chunk_up = carve(NCH * T)
        chunk_dn = carve(NCH * T)
        assert WS >= 4 * D
        xn = slot[1][:, 0:2 * D].rearrange("p (i d) -> p i d", i=2)
        xnt = slot[1][:, 2 * D:4 * D].rearrange("p (k c) -> p k c", k=KD)
        visits_f = slot[1][:, 0:3 * MAXV].rearrange("p (a v) -> p a v", a=3)
        tmp320 = slot[1][:, 3 * MAXV:3 * MAXV + 2 * NCH * T].rearrange("p (a n) -> p a n", a=2)
        at[0] = g_at
        gath = [carve(T * HID).rearrange("p (t n) -> p t n", t=T) for _ in range(2)]
        wgt = carve(T * HEADS * SLOT).rearrange("p (t n) -> p t n", t=T)
        lrelu_t = carve(T * HID).rearrange("p (b n) -> p b n", b=2)
        oh_e = carve(T * P).rearrange("p (t n) -> p t n", t=T)
        oh_d = [carve(CH, BF16) for _ in range(2)]
        mask = carve(CH, BF16)
        drow = carve(CH, I32)
        idx = [carve(T, I32) for _ in range(2)]
        e_row = carve(CH).rearrange("p (b n) -> p b n", b=2)
        e_row_b = carve(CH, BF16).rearrange("p (b n) -> p b n", b=2)
        score_r = carve(2 * HEADS * HT * P, BF16).rearrange("p (b n) -> p b n", b=2)
        fold = carve(HEADS * HT * P, BF16).rearrange("p (h n) -> p h n", h=HEADS)
        dcol_c = [carve(T) for _ in range(2)]
        z_e = carve(T * HEADS)
        cmax = carve(HEADS)
        m_neg = carve(HEADS, BF16)
        m_n = carve(HEADS)
        m_d = carve(HEADS)
        m_s = carve(HEADS)
        graph_end = at[0]
        at[0] = 0
        ht = carve(KD * NT * P).rearrange("p (k c) -> p k c", k=KD)
        slot += [carve(WS), carve(WS)]
        wu_s = slot[2].rearrange("p (k n) -> p k n", k=KD)
        wd_s = slot[3].rearrange("p (k n) -> p k n", k=KI)
        f_at = at[0]
        o_s = carve(2 * HID).rearrange("p (i n) -> p i n", i=2)
        o_t = carve(KH * GT).rearrange("p (k c) -> p k c", k=KH)
        rden = carve(2 * HEADS).rearrange("p (i h) -> p i h", i=2)
        h_s = carve(2 * D).rearrange("p (i d) -> p i d", i=2)
        at[0] = f_at
        qt = carve(HEADS * GT).rearrange("p (j c) -> p j c", j=HEADS)
        sim = carve(2 * KEYP * NK).rearrange("p (i a n) -> p i a n", i=2, a=KEYP)
        sg = carve(KI * GT)
        a_t = carve(KI * GT).rearrange("p (k c) -> p k c", k=KI)
        COMP = 2 * HEADS * NK + 2 * HEADS * NX + 1
        comp = carve(COMP)
        s8 = carve(KEYP * TOP).rearrange("p (a n) -> p a n", a=KEYP)
        i8 = carve(KEYP * TOP, U32).rearrange("p (a n) -> p a n", a=KEYP)
        i8f = carve(KEYP * TOP).rearrange("p (a n) -> p a n", a=KEYP)
        e8 = carve(KEYP * TOP).rearrange("p (a n) -> p a n", a=KEYP)
        grid = carve(HEADS * TOP * TOP)
        grid_r = carve(HEADS * TOP * TOP)
        sel = carve(HEADS * TOP * TOP)
        wsel = carve(HEADS * TOP * TOP)
        g8 = carve(HEADS * TOP).rearrange("p (h n) -> p h n", h=HEADS)
        n_i = carve(HEADS * TOP)
        r_i = carve(HEADS * TOP)
        z_h = carve(HEADS)
        rz = carve(HEADS)
        eq = carve(HEADS * NK)
        at[0] = f_at
        cmp_in = carve(2 * COMP).rearrange("p (i n) -> p i n", i=2)
        s_q = carve(2 * EB * NK).rearrange("p (i b n) -> p i b n", i=2, b=EB)
        s_tmp = carve(EB * HEADS * NK).rearrange("p (b h n) -> p b h n", b=EB, h=HEADS)
        s_t = carve(EB * GT).rearrange("p (b c) -> p b c", b=EB)
        sd_t = carve(EB * GT).rearrange("p (b c) -> p b c", b=EB)
        v_t = carve(EB * GT).rearrange("p (b c) -> p b c", b=EB)

        def parts(c):
            a, b = HEADS * NK, HEADS * NX
            return (c[:, 0:a].rearrange("p (h n) -> p h n", h=HEADS),
                    c[:, a:2 * a].rearrange("p (h n) -> p h n", h=HEADS),
                    c[:, 2 * a:2 * a + b].rearrange("p (h n) -> p h n", h=HEADS),
                    c[:, 2 * a + b:2 * a + 2 * b].rearrange("p (h n) -> p h n", h=HEADS),
                    c[:, COMP - 1:COMP])

        ps = ctx.enter_context(nc.psum_tensor("ps", [P, 8, 512], F32))

        def banks(a, n=1):
            return ps[:, a:a + n, :].rearrange("p b n -> p (b n)")

        ROW_BANK = (4, 6, 5)
        xl_dram = nc.dram_tensor("xl_rows", (NT * P, HID), F32, kind="Internal").ap()
        comp_dram = nc.dram_tensor("comp_rows", (NT, P, COMP), F32, kind="Internal").ap()

        x_pad0 = sem("x_pad0")
        x_in = sem("x_in")
        x_tail = sem("x_tail")
        gw_in = sem("gw_in")
        ew_in = sem("ew_in")
        const_ready = sem("const_ready")
        wdn_scaled = sem("wdn_scaled")
        var_ready = sem("var_ready")
        sd_ready = sem("sd_ready")
        xn_ready = sem("xn_ready")
        xnt_ps = sem("xnt_ps")
        xnt_ready = sem("xnt_ready")
        zt_ps = sem("zt_ps")
        zt_ready = sem("zt_ready")
        xlr_ps = sem("xlr_ps")
        xl_ready = sem("xl_ready")
        attb_zero = sem("attb_zero")
        attb_in = sem("attb_in")
        xl_out = sem("xl_out")
        bnd_ready = sem("bnd_ready")
        bnd_ps = sem("bnd_ps")
        sz_ready = sem("sz_ready")
        sp_ready = sem("sp_ready")
        tab_ready = sem("tab_ready")
        drow_in = sem("drow_in")
        idx_in = [sem("idx_in_0"), sem("idx_in_1")]
        drow_free = sem("drow_free")
        idx_free = sem("idx_free")
        idx_seen = sem("idx_seen")
        g_in = [[sem("g_in_0a"), sem("g_in_0b")], [sem("g_in_1a"), sem("g_in_1b")]]
        g_free = [sem("g_free_a"), sem("g_free_b")]
        ohd_ready = sem("ohd_ready")
        mask_ready = sem("mask_ready")
        mw_ready = sem("mw_ready")
        msg_ps = [sem("msg_ps_a"), sem("msg_ps_b")]
        scaled_ready = [sem("scaled_ready_a"), sem("scaled_ready_b")]
        lrelu_ready = [sem("lrelu_ready_a"), sem("lrelu_ready_b")]
        e_ps = [sem("e_ps_a"), sem("e_ps_b")]
        e_copied = [sem("e_copied_a"), sem("e_copied_b")]
        bc_ps = sem("bc_ps")
        bc_copied = sem("bc_copied")
        fold_done = sem("fold_done")
        m_ready = sem("m_ready")
        z_ps = sem("z_ps")
        ms_ready = sem("ms_ready")
        z_ready = sem("z_ready")
        p_ready = sem("p_ready")
        wg_ready = [sem("wg_ready_a"), sem("wg_ready_b")]
        sc_ps = sem("sc_ps")
        phase_done = sem("phase_done")
        fw_in = sem("fw_in")
        fw2_in = sem("fw2_in")
        keys_zero = sem("keys_zero")
        o_ready = sem("o_ready")
        ot_ps = sem("ot_ps")
        ot_ready = sem("ot_ready")
        y_ps = sem("y_ps")
        x1_ready = sem("x1_ready")
        var2_ready = sem("var2_ready")
        sd2_ready = sem("sd2_ready")
        h_ready = sem("h_ready")
        ht_ps = sem("ht_ps")
        ht_ready = sem("ht_ready")
        q_ps = sem("q_ps")
        g_ps = sem("g_ps")
        u_ps = sem("u_ps")
        qt_ready = sem("qt_ready")
        silu_ready = sem("silu_ready")
        at_ready = sem("at_ready")
        sim_ps = sem("sim_ps")
        sim_ready = sem("sim_ready")
        sim_free = sem("sim_free")
        mlp_ps = sem("mlp_ps")
        mlp_added = sem("mlp_added")
        ex_in_ready = sem("ex_in_ready")
        ex_ready = sem("ex_ready")
        comp_ready = sem("comp_ready")
        comp_out = sem("comp_out")
        cmp_in_s = [sem("cmp_in_0"), sem("cmp_in_1")]
        cmp_free = sem("cmp_free")
        dw_in = [sem("dw_in_0"), sem("dw_in_1")]
        s_ready = sem("s_ready")
        st_ps = sem("st_ps")
        st_ready = sem("st_ready")
        d_ps = sem("d_ps")
        sd_act = sem("sd_act")
        v_ready = sem("v_ready")
        yx_ps = sem("yx_ps")
        yx_added = sem("yx_added")
        out_done = sem("out_done")

        block = ctx.enter_context(nc.Block())

        def phase(eng, n):
            eng.drain()
            eng.sem_inc(phase_done, 1)
            eng.wait_ge(phase_done, 5 * n)

        def run_visits(eng, front, both, last):
            later = eng.value_load(n_pairs[0:1, 1:2], min_val=NT // 2 - 1, max_val=MAXV // 2 - 2)
            front(0, 0, 0)
            with eng.Fori(0, later) as i:
                both(1, 2 * i + 1, i, 2 * i)
                both(0, 2 * i + 2, i + 1, 2 * i + 1)
            both(1, 2 * later + 1, later, 2 * later)
            last(2 * later + 1)

        def run_experts(eng, first, both, last):
            for q in range(QE):
                if q == 0:
                    first(0, 0, 0)
                else:
                    both(NG * q, q, 0, NG - 1)
                with eng.Fori(0, NG - 1) as g:
                    both(g + (NG * q + 1), q, g + 1, g)
            last(NG - 1)

        def window_of(eng, v):
            return eng.value_load(visits[0:1, 0, bass.ds(v, 1)], min_val=0, max_val=NT)

        def chunk_of(eng, v):
            return eng.value_load(visits[0:1, 1, bass.ds(v, 1)], min_val=0, max_val=NCH - 1)

        @block.sync
        def _(sp):
            sp.dma_start(xs[:, 0:NT - 1, :], x[0:(NT - 1) * P, :].rearrange("(t p) d -> p t d", p=P)).then_inc(x_in, 16)
            sp.wait_ge(x_pad0, 1)
            sp.dma_start(xs[0:LAST, NT - 1, :], x[(NT - 1) * P:N, :]).then_inc(x_tail, 16)
            sp.dma_start(wdn_s, w_down.rearrange("(k p) n -> p k n", p=P)).then_inc(gw_in, 16)
            sp.dma_start(rms_s, rms_w).then_inc(gw_in, 16)
            sp.dma_start(wlr_s[:, :, 0:HID], w_l.rearrange("(k p) n -> p k n", p=P)).then_inc(gw_in, 16)
            sp.dma_start(wlr_s[:, :, HID:2 * HID], w_r.rearrange("(k p) n -> p k n", p=P)).then_inc(gw_in, 16)
            sp.dma_start(att_s, att.rearrange("(o h) d -> o (h d)", o=1).broadcast_to((P, HID))).then_inc(ew_in, 16)
            sp.dma_start(dst_i.rearrange("p (c t) -> p c t", t=T), dst.rearrange("(c p t) -> p c t", p=P, t=T)).then_inc(ew_in, 16)
            sp.wait_ge(attb_zero, 1)
            with nc.allow_non_contiguous_dma(reason="256 numbers once"):
                for h in range(HEADS):
                    r = (h % 2) * HD
                    sp.dma_start(att_b[r:r + HD, h // 2, h:h + 1], att[h:h + 1, :].rearrange("o d -> d o")).then_inc(attb_in, 16)
            sp.dma_start(wup_s[:], w_up.rearrange("(k p) n -> p k n", p=P)).then_inc(fw_in, 16)
            sp.dma_start(wq_s, wq_t.rearrange("(k p) n -> p k n", p=P)).then_inc(fw_in, 16)
            sp.wait_ge(keys_zero, 1)
            for r in range(2):
                for a in range(2):
                    sp.dma_start(keys_s[QH * r:QH * r + QH, 2 * a:2 * a + 2, r, :],
                                 keys_t[:, a, r::2, :]).then_inc(fw_in, 16)
            sp.wait_ge(xl_ready, 1)
            sp.dma_start(xl_dram.rearrange("(t p) n -> p t n", p=P), xl).then_inc(xl_out, 16)
            phase(sp, 1)
            sp.dma_start(wg_s, wg_t.rearrange("(k p) n -> p k n", p=P)).then_inc(fw_in, 16)

            def sp_front(par, v, n, before=None):
                c = chunk_of(sp, v)
                sp.wait_ge(idx_seen, v + 1)
                sp.wait_ge(idx_free, v + 1)
                sp.dma_start(idx[par], src[bass.ds(c * CH, CH)].rearrange("(p t) -> p t", t=T)).then_inc(idx_in[par], 16)
                sp.wait_ge(drow_free, v + 1)
                sp.dma_start(drow, dst[bass.ds(c * CH, CH)].rearrange("(o n) -> o n", o=1).broadcast_to((P, CH)))\
                    .then_inc(drow_in, 16)

            run_visits(sp, sp_front, sp_front, lambda v: None)
            phase(sp, 2)
            sp.dma_start(wu_s, wu_t.rearrange("(k p) n -> p k n", p=P)).then_inc(fw2_in, 16)
            sp.dma_start(wd_s, wd_t.rearrange("(k p) n -> p k n", p=P)).then_inc(fw2_in, 16)
            sp.wait_ge(fw2_in, 32)
            phase(sp, 3)
            with sp.Fori(0, NT) as t:
                sp.wait_ge(comp_ready, t + 1)
                sp.dma_start(comp_dram[bass.ds(t, 1), :, :].rearrange("o p n -> p (o n)"), comp).then_inc(comp_out, 16)
            sp.wait_ge(comp_out, 16 * NT + 16)
            phase(sp, 4)

            for q in range(QE):
                with sp.Fori(0, NG) as g:
                    for i in range(2):
                        sp.wait_ge(cmp_free, 2 * NG * q + 2 * g + i + 1)
                        sp.dma_start(cmp_in[:, i, :], comp_dram[bass.ds(2 * g + i, 1), :, :].rearrange("o p n -> p (o n)"))\
                            .then_inc(cmp_in_s[i], 16)
            sp.wait_ge(yx_added, NG * QE + 1)
            sp.dma_start(out[0:(NT - 1) * P, :].rearrange("(t p) d -> p t d", p=P), xs[:, 0:NT - 1, :]).then_inc(out_done, 16)
            sp.dma_start(out[(NT - 1) * P:N, :], xs[0:LAST, NT - 1, :]).then_inc(out_done, 16)
            sp.wait_ge(out_done, 32)

        @block.gpsimd
        def _(pool):
            pool.memset(xs[:, NT - 1, :], 0.0).then_inc(x_pad0, 1)
            pool.memset(keys_s[:], 0.0).then_inc(keys_zero, 1)
            pool.memset(zero_pool[:], 0)
            pool.memset(att_b, 0.0).then_inc(attb_zero, 1)
            pool.memset(ident[:], 0.0).then_inc(const_ready, 1)
            pool.memset(ident_b[:], 0.0).then_inc(const_ready, 1)
            pool.wait_ge(const_ready, 2)
            for m in (ident, ident_b):
                pool.affine_select(out=m[:], in_=m[:], compare_op=ALU.not_equal, fill=1.0, base=0,
                                   pattern=[[-1, P]], channel_multiplier=1).then_inc(const_ready, 1)
            kw = dict(allow_small_or_imprecise_dtypes=True)
            pool.iota(iota_row[:], [[1, P]], base=0, channel_multiplier=0, **kw).then_inc(const_ready, 1)
            pool.iota(iota_part[:], [[0, 1]], base=0, channel_multiplier=1, **kw).then_inc(const_ready, 1)
            pool.iota(win_base[:], [[P, NT + 1]], base=0, channel_multiplier=0, **kw).then_inc(const_ready, 1)
            pool.iota(chunk_up.rearrange("p (c t) -> p c t", t=T), [[1, NCH], [0, T]], base=1, channel_multiplier=0, **kw)\
                .then_inc(const_ready, 1)
            pool.iota(chunk_dn.rearrange("p (c t) -> p c t", t=T), [[-1, NCH], [0, T]], base=NCH, channel_multiplier=0, **kw)\
                .then_inc(const_ready, 1)
            pool.iota(win_node[:], [[P, NT + 1]], base=0, channel_multiplier=1, **kw).then_inc(const_ready, 1)
            pool.iota(visits_n, [[1, MAXV]], base=0, channel_multiplier=0, **kw).then_inc(const_ready, 1)
            pool.wait_ge(const_ready, 11)
            pool.wait_ge(xl_out, 16)
            pool.sem_inc(idx_seen, 2)
            phase(pool, 1)

            def pool_front(par, v, n, before=None):
                for b in range(2):
                    if b == 0:
                        pool.wait_ge(idx_in[par], 16 * n + 16)
                    pool.wait_ge(g_free[b], v + 1)
                    pace = pool.tensor_tensor(pace_pool[:, 2 * par + b:2 * par + b + 1], zero_pool[:], zero_pool[:], ALU.add)
                    if b == 1:
                        pace.then_inc(idx_seen, 1)
                    for t in range(b * HT, b * HT + HT):
                        pool.indirect_dma_start(gath[par][:, t, :], None, xl_dram[:, :],
                                                bass.IndirectOffsetOnAxis(ap=idx[par][:, t:t + 1], axis=0)).then_inc(g_in[par][b], 16)

            run_visits(pool, pool_front, pool_front, lambda v: None)
            for n in (2, 3, 4):
                phase(pool, n)

            def experts(q):
                b = q % 2
                pool.dma_start(slot[2 * b][:, :].rearrange("p (k n) -> p k n", k=KD),
                             down_t[:, q * EB * P:(q + 1) * EB * P].rearrange("(k p) n -> p k n", p=P)).then_inc(dw_in[b], 16)
                pool.dma_start(slot[2 * b + 1][:, :].rearrange("p (k n) -> p k n", k=EB),
                             up[q * EB * P:(q + 1) * EB * P, :].rearrange("(k p) n -> p k n", p=P)).then_inc(dw_in[b], 16)

            for q in range(QE):
                if q >= 2:
                    pool.wait_ge(yx_ps, NG * (q - 1))
                experts(q)

        @block.scalar
        def _(act):
            act.sem_inc(xnt_ready, 1)
            act.wait_ge(var_ready, 1)
            act.activation(nrm[:, 1, :], nrm[:, 0, :], ACT.Sqrt).then_inc(sd_ready, 1)
            act.wait_ge(var_ready, 2)
            act.activation(nrm[:, 3, :], nrm[:, 2, :], ACT.Sqrt).then_inc(sd_ready, 1)
            with act.Fori(0, NG) as g:
                act.wait_ge(xnt_ps, g + 1)
                act.activation(xnt.rearrange("p k c -> p (k c)"), banks(0, 4), ACT.Copy).then_inc(xnt_ready, 1)
            act.wait_ge(sz_ready, 1)
            act.activation(p_self, p_self, ACT.Exp).then_inc(sp_ready, 1)
            act.wait_ge(tab_ready, 1)
            phase(act, 1)

            def act_front(par, v, n):
                for b in range(2):
                    act.wait_ge(msg_ps[b], v + 1)
                    act.activation(lrelu_t[:, b, :], banks(2 * b, 2), ACT.Copy, scale=0.2).then_inc(scaled_ready[b], 1)
                for b in range(2):
                    act.wait_ge(e_ps[b], v + 1)
                    act.activation(e_row_b[0:HEADS, b, :], ps[0:HEADS, 4 + b, :], ACT.Copy)
                    act.activation(e_row[0:HEADS, b, :], ps[0:HEADS, 4 + b, :], ACT.Copy).then_inc(e_copied[b], 1)
                act.wait_ge(fold_done, v + 1)
                for k in range(2 * HEADS):
                    act.wait_ge(bc_ps, 8 * v + k + 1)
                    act.activation(score_r[:, k // HEADS, (k % HEADS) * HT * P:(k % HEADS + 1) * HT * P], banks(ROW_BANK[k % 3]), ACT.Copy)\
                        .then_inc(bc_copied, 1)

            def act_back(v):
                act.wait_ge(m_ready, v + 1)
                act.activation(m_s, m_d, ACT.Exp).then_inc(ms_ready, 1)
                act.wait_ge(z_ready, v + 1)
                act.activation(wgt.rearrange("p t (h s) -> p (t h) s", s=SLOT)[:, :, HD], z_e, ACT.Exp).then_inc(p_ready, 1)

            def act_both(par, v, n, before):
                act_back(before)
                act_front(par, v, n)

            run_visits(act, act_front, act_both, act_back)
            phase(act, 2)
            with act.Fori(0, NG) as g:
                act.wait_ge(ot_ps, g + 1)
                act.activation(o_t.rearrange("p k c -> p (k c)"), banks(0), ACT.Copy).then_inc(ot_ready, 1)
            act.wait_ge(var2_ready, 1)
            act.activation(nrm[:, 1, :], nrm[:, 0, :], ACT.Sqrt).then_inc(sd2_ready, 1)
            with act.Fori(0, NG) as g:
                act.wait_ge(ht_ps, g + 1)
                act.activation(pace_act[:], iota_part[:], ACT.Copy)
                act.activation(ht[:, :, bass.ds(g * GT, GT)], banks(0, 4).rearrange("p (k c) -> p k c", k=KD), ACT.Copy)
                act.drain()
                act.sem_inc(ht_ready, 1)
            phase(act, 3)
            act.sem_inc(qt_ready, 1)
            act.sem_inc(sim_ready, 2)
            with act.Fori(0, NG) as g:
                act.wait_ge(q_ps, g + 1)
                act.activation(qt.rearrange("p j c -> p (j c)"), banks(0, 2), ACT.Copy).then_inc(qt_ready, 1)
                act.wait_ge(g_ps, g + 1)
                act.activation(sg, banks(2, 2), ACT.Silu).then_inc(silu_ready, 1)
                for i in range(2):
                    act.wait_ge(sim_ps, 2 * g + i + 1)
                    act.wait_ge(sim_free, 2 * g + i + 1)
                    act.activation(sim[:, i, :, :].rearrange("p a n -> p (a n)"), banks(6 * (1 - i), 2), ACT.Copy)\
                        .then_inc(sim_ready, 1)
                for i in range(2):
                    ey, rr, thr, ex, cl = parts(comp)
                    act.wait_ge(ex_in_ready, 2 * g + i + 1)
                    act.activation(ey, ey, ACT.Exp)
                    act.activation(ex, ex, ACT.Exp)
                    act.activation(e8.rearrange("p a n -> p (a n)"), e8.rearrange("p a n -> p (a n)"), ACT.Exp)\
                        .then_inc(ex_ready, 1)
            phase(act, 4)
            act.sem_inc(st_ready, 1)
            act.sem_inc(sd_act, 1)
            for q in range(QE):
                with act.Fori(0, NG) as g:
                    act.wait_ge(v_ready, NG * q + g + 1)
                    act.wait_ge(d_ps, NG * q + g + 1)
                    act.activation(sd_t.rearrange("p b c -> p (b c)"), banks(2, 2), ACT.Silu).then_inc(sd_act, 1)
                    act.wait_ge(st_ps, NG * q + g + 1)
                    act.activation(s_t.rearrange("p b c -> p (b c)"), banks(0, 2), ACT.Copy).then_inc(st_ready, 1)

        @block.vector
        def _(dve):
            dve.wait_ge(x_in, 16)
            dve.wait_ge(x_tail, 16)

            def all_stats():
                with dve.Fori(0, NT) as t:
                    for a in range(2):
                        dve.bn_stats(stats[:, bass.ds(t, 1), a, :].rearrange("p o s -> p (o s)"),
                                     xs[:, bass.ds(t, 1), a * 512:a * 512 + 512].rearrange("p o d -> p (o d)"))
                dve.drain()
                for t in range(NT):
                    dve.bn_aggr(meanvar[:, t, :], stats[:, t, :, :].rearrange("p a s -> p (a s)"))
                dve.drain()

            all_stats()
            dve.tensor_scalar(nrm[:, 0, :], meanvar[:, :, 1], 1e-5, None, ALU.add).then_inc(var_ready, 1)
            dve.wait_ge(sd_ready, 1)
            dve.reciprocal(nrm[:, 1, :], nrm[:, 1, :])
            dve.drain()
            dve.tensor_tensor(nrm[:, 2, :], nrm[:, 1, :], nrm[:, 1, :], ALU.mult)
            dve.drain()
            dve.tensor_tensor(nrm[:, 2, :], nrm[:, 2, :], meanvar[:, :, 1], ALU.mult)
            dve.drain()
            dve.tensor_scalar(nrm[:, 2, :], nrm[:, 2, :], 1e-6, None, ALU.add).then_inc(var_ready, 1)
            dve.wait_ge(gw_in, 64)
            for k in range(KD):
                last = dve.tensor_scalar(wdn_s[:, k, :], wdn_s[:, k, :], rms_s[:, k:k + 1], None, ALU.mult)
            last.then_inc(wdn_scaled, 1)
            dve.wait_ge(sd_ready, 2)
            dve.reciprocal(nrm[:, 3, :], nrm[:, 3, :])
            dve.drain()
            dve.tensor_tensor(nrm[:, 3, :], nrm[:, 3, :], nrm[:, 1, :], ALU.mult)
            dve.drain()
            with dve.Fori(0, NG) as g:
                dve.wait_ge(xnt_ready, g + 1)
                for i in range(2):
                    t = bass.ds(2 * g + i, 1)
                    last = dve.tensor_scalar(xn[:, i, :], xs[:, t, :].rearrange("p o d -> p (o d)"),
                                             meanvar[:, t, 0], nrm[:, 3, t], ALU.subtract, ALU.mult)
                last.then_inc(xn_ready, 1)
                dve.wait_ge(zt_ps, g + 1)
                dve.tensor_copy(zt.rearrange("p k c -> p (k c)"), banks(4)).then_inc(zt_ready, 1)
                dve.wait_ge(xlr_ps, g + 1)
                dve.tensor_scalar(xl[:, bass.ds(2 * g, 2), :], ps[:, 5:7, 0:HID], 1.0, None, ALU.mult)
                dve.tensor_scalar(xr[:, bass.ds(2 * g, 2), :], ps[:, 5:7, HID:2 * HID], 1.0, None, ALU.mult)
            dve.drain()
            dve.sem_inc(xl_ready, 1)
            dve.wait_ge(ew_in, 32)
            att_r = att_s.rearrange("p (o n) -> p o n", o=1).broadcast_to((P, NT, HID))
            dve.tensor_tensor(s_res, xl, xr, ALU.add)
            dve.drain()
            dve.scalar_tensor_tensor(s_res, s_res, 0.2, s_res, ALU.mult, ALU.max)
            dve.drain()
            dve.tensor_tensor(s_res, s_res, att_r, ALU.mult)
            dve.drain()
            dve.tensor_reduce(e_self, s_res.rearrange("p t (h d) -> p (t h) d", h=HEADS), AX.X, ALU.add)
            dve.drain()
            dve.tensor_copy(m_self, e_self)
            dve.memset(m_all[:, NT, :], 0.0)
            dve.memset(acc_all[:, NT, :, :], 0.0)
            dve.memset(xr3[:, NT, :, :], 0.0)
            dve.drain()
            dve.tensor_copy(m_all[:, 0:NT, :].rearrange("p t h -> p (t h)"), m_self)
            dve.tensor_tensor(p_self, e_self, m_self, ALU.subtract).then_inc(sz_ready, 1)
            dve.tensor_copy(xr3[:, 0:NT, 0, :], xr)
            dve.drain()
            dve.tensor_tensor(s_res, xr, xr3[:, 0:NT, 0, :], ALU.subtract)
            dve.drain()
            dve.tensor_copy(xr3[:, 0:NT, 1, :], s_res)
            dve.drain()
            dve.tensor_tensor(xr3[:, 0:NT, 2, :], s_res, xr3[:, 0:NT, 1, :], ALU.subtract)
            dve.wait_ge(sp_ready, 1)
            p_b = p_self.rearrange("p (t h o) -> p t h o", h=HEADS, o=1)
            for t in range(NT):
                dve.tensor_tensor(acc_all[:, t, :, 0:HD], xl[:, t, :].rearrange("p (h d) -> p h d", h=HEADS),
                                  p_b[:, t, :, :].broadcast_to((P, HEADS, HD)), ALU.mult)
            dve.tensor_copy(acc_all[:, 0:NT, :, :].rearrange("p t h s -> p (t h) s")[:, :, HD], p_self)
            dve.wait_ge(const_ready, 11)
            dve.tensor_copy(dcol, dst_i)
            dve.drain()
            for w in range(NT):
                dve.tensor_scalar(tmp320[:, 0, :], dcol, float(w * P), None, ALU.is_ge)
                dve.drain()
                dve.scalar_tensor_tensor(tmp320[:, 0, :], dcol, float(w * P + P), tmp320[:, 0, :], ALU.is_lt, ALU.mult)
                dve.drain()
                dve.tensor_tensor_reduce(tmp320[:, 1, :], tmp320[:, 0, :], chunk_up, 1.0, 0.0, ALU.mult, ALU.max,
                                         bnd_p[:, w:w + 1])
                dve.drain()
                dve.tensor_tensor_reduce(tmp320[:, 1, :], tmp320[:, 0, :], chunk_dn, 1.0, 0.0, ALU.mult, ALU.max,
                                         bnd_p[:, NT + w:NT + w + 1])
                dve.drain()
            dve.sem_inc(bnd_ready, 1)
            dve.wait_ge(bnd_ps, 1)
            dve.tensor_reduce(bnd_t[0:2 * NT, 0:1], ps[0:2 * NT, 7, 0:P], AX.X, ALU.max).then_inc(bnd_ready, 1)
            dve.wait_ge(bnd_ps, 2)
            r0 = bnd_r[0:1, :, :]
            dve.tensor_scalar(r0[:, 1, :], ps[0:1, 7, P:P + NT], 1.0, None, ALU.max)
            dve.tensor_scalar(r0[:, 0, :], ps[0:1, 7, P + NT:P + 2 * NT], -1.0, float(NCH), ALU.mult, ALU.add)
            dve.drain()
            dve.tensor_scalar(r0[:, 2, :], r0[:, 1, :], -1.0, None, ALU.add)
            dve.drain()
            dve.tensor_tensor(r0[:, 0, :], r0[:, 0, :], r0[:, 2, :], ALU.min)
            dve.drain()
            dve.tensor_tensor(r0[:, 2, :], r0[:, 1, :], r0[:, 0, :], ALU.subtract)
            dve.memset(r0[:, 3, 0:1], 1.0)
            dve.drain()
            for w in range(NT - 1):
                dve.tensor_tensor(r0[:, 3, w + 1:w + 2], r0[:, 3, w:w + 1], r0[:, 2, w:w + 1], ALU.add)
                dve.drain()
            dve.tensor_tensor(r0[:, 1, :], r0[:, 0, :], r0[:, 3, :], ALU.subtract)
            dve.tensor_tensor(r0[:, 4, 0:1], r0[:, 3, NT - 1:NT], r0[:, 2, NT - 1:NT], ALU.add)
            dve.drain()
            vn, vf = visits_n[0:1, :], visits_f[0:1, :, :]
            dve.memset(vf[:, 0, :], 0.0)
            dve.tensor_scalar(vf[:, 1, :], vn, r0[:, 1, 0:1], 1.0, ALU.add, ALU.add)
            dve.tensor_tensor(bnd_r[0:1, 2, 1:NT], r0[:, 1, 1:NT], r0[:, 1, 0:NT - 1], ALU.subtract)
            dve.drain()
            for w in range(1, NT):
                dve.tensor_scalar(vf[:, 2, :], vn, 1.0, r0[:, 3, w:w + 1], ALU.add, ALU.is_ge)
                dve.drain()
                dve.tensor_tensor(vf[:, 0, :], vf[:, 0, :], vf[:, 2, :], ALU.add)
                dve.scalar_tensor_tensor(vf[:, 1, :], vf[:, 2, :], r0[:, 2, w:w + 1], vf[:, 1, :], ALU.mult, ALU.add)
                dve.drain()
            dve.tensor_scalar(vf[:, 2, :], vn, 1.0, r0[:, 4, 0:1], ALU.add, ALU.is_lt)
            dve.drain()
            dve.tensor_tensor(vf[:, 1, :], vf[:, 1, :], vf[:, 2, :], ALU.mult)
            dve.tensor_scalar(vf[:, 0, :], vf[:, 0, :], float(-NT), None, ALU.add)
            dve.drain()
            dve.tensor_tensor(vf[:, 0, :], vf[:, 0, :], vf[:, 2, :], ALU.mult)
            dve.tensor_scalar(r0[:, 4, 1:2], r0[:, 4, 0:1], 0.5, None, ALU.mult)
            dve.drain()
            dve.tensor_scalar(vf[:, 0, :], vf[:, 0, :], float(NT), None, ALU.add)
            dve.tensor_scalar(vf[:, 2, :], vn, 1.0, r0[:, 4, 1:2], ALU.add, ALU.is_le)
            dve.drain()
            dve.tensor_reduce(r0[:, 4, 2:3], vf[:, 2, :], AX.X, ALU.add)
            dve.tensor_copy(visits[0:1, :, :], vf[:, 0:2, :])
            dve.drain()
            dve.tensor_scalar(n_pairs[0:1, 1:2], r0[:, 4, 2:3], -1.0, None, ALU.add)
            dve.drain()
            dve.tensor_copy(n_pairs[0:1, 0:1], r0[:, 4, 2:3]).then_inc(tab_ready, 1)
            for s in (drow_free, idx_free, idx_free, *g_free, *g_free, fold_done):
                dve.sem_inc(s, 1)
            phase(dve, 1)

            def dve_one_hots(par, v):
                w, c = window_of(dve, v), chunk_of(dve, v)
                dve.wait_ge(drow_in, 16 * v + 16)
                dve.tensor_scalar(oh_d[par], drow, win_node[:, bass.ds(w, 1)], None, ALU.is_equal).then_inc(ohd_ready, 1)
                dve.tensor_scalar(dcol_c[par], dcol[:, bass.ds(c * T, T)], win_base[:, bass.ds(w, 1)], None, ALU.subtract)
                dve.drain()
                dve.sem_inc(drow_free, 1)

            def dve_maxima(v):
                w = window_of(dve, v)
                m_wv = m_all[:, bass.ds(w, 1), :].rearrange("p o h -> p (o h)")
                n = HT * P
                dve.wait_ge(bc_copied, 8 * v + 8)
                dve.tensor_tensor(fold.rearrange("p h n -> p (h n)"), score_r[:, 0, :], score_r[:, 1, :], ALU.max)
                dve.drain()
                dve.sem_inc(fold_done, 1)
                for q in (2, 4):
                    dve.tensor_tensor(fold[:, :, 0:n // q], fold[:, :, 0:n // q], fold[:, :, n // q:2 * n // q], ALU.max)
                    dve.drain()
                dve.tensor_reduce(cmax, fold[:, :, 0:n // 4], AX.X, ALU.max)
                dve.drain()
                dve.tensor_tensor(m_n, cmax, m_wv, ALU.max)
                dve.drain()
                dve.tensor_scalar(m_neg, m_n, -1.0, None, ALU.mult).then_inc(mw_ready, 1)
                dve.tensor_tensor(m_d, m_wv, m_n, ALU.subtract).then_inc(m_ready, 1)
                dve.drain()
                dve.tensor_copy(m_wv, m_n)

            def dve_exponents(v):
                dve.wait_ge(z_ps, v + 1)
                dve.tensor_scalar(z_e, ps[:, 7, SUMS:SUMS + T * HEADS], 80.0, None, ALU.min).then_inc(z_ready, 1)

            def dve_weigh(par, v, b):
                h = slice(b * HT, (b + 1) * HT)
                wv = wgt[:, h, :].rearrange("p t (h s) -> p (t h) s", s=SLOT)
                if b == 0:
                    dve.wait_ge(p_ready, v + 1)
                dve.tensor_tensor(wv[:, :, 0:HD], gath[par][:, h, :].rearrange("p t (h d) -> p (t h) d", h=HEADS),
                                  wv[:, :, HD:SLOT].broadcast_to((P, HT * HEADS, HD)), ALU.mult).then_inc(wg_ready[b], 1)
                dve.drain()
                dve.sem_inc(g_free[b], 1)
                if b == 1:
                    dve.sem_inc(idx_free, 1)

            def dve_lrelu(v, b):
                dve.wait_ge(scaled_ready[b], v + 1)
                dve.tensor_tensor(lrelu_t[:, b, :], lrelu_t[:, b, :], banks(2 * b, 2), ALU.max).then_inc(lrelu_ready[b], 1)

            def dve_mask(par, v):
                dve.tensor_scalar(mask, oh_d[par], -1.0, BIG, ALU.add, ALU.mult).then_inc(mask_ready, 1)

            def dve_sums(v):
                w = window_of(dve, v)
                av = acc_all[:, bass.ds(w, 1), :, :].rearrange("p o h s -> p (o h) s")
                dve.wait_ge(ms_ready, v + 1)
                dve.tensor_tensor(av, av, m_s.rearrange("p (h o) -> p h o", o=1).broadcast_to((P, HEADS, SLOT)), ALU.mult)
                dve.drain()
                dve.wait_ge(sc_ps, v + 1)
                dve.tensor_tensor(av, av, ps[:, 7, 0:HEADS * SLOT].rearrange("p (h s) -> p h s", h=HEADS), ALU.add)
                dve.drain()

            def dve_edge_hots(par):
                for t in range(T):
                    last = dve.tensor_scalar(oh_e[:, t, :], iota_row[:], dcol_c[par][:, t:t + 1], None, ALU.is_equal)

            def dve_front(par, v, n):
                dve_one_hots(par, v)
                dve_lrelu(v, 0)
                dve_lrelu(v, 1)
                dve_mask(par, v)
                dve_edge_hots(par)

            def dve_both(par, v, n, before):
                dve_one_hots(par, v)
                dve_maxima(before)
                dve_exponents(before)
                dve_weigh(1 - par, before, 0)
                dve_weigh(1 - par, before, 1)
                dve_lrelu(v, 0)
                dve_lrelu(v, 1)
                dve_mask(par, v)
                dve_sums(before)
                dve_edge_hots(par)

            def dve_last(v):
                dve_maxima(v)
                dve_exponents(v)
                dve_weigh(1, v, 0)
                dve_weigh(1, v, 1)
                dve_sums(v)

            run_visits(dve, dve_front, dve_both, dve_last)
            phase(dve, 2)

            with dve.Fori(0, NG) as g:
                t2 = bass.ds(2 * g, 2)
                dve.tensor_scalar(rden, acc_all[:, t2, :, HD], 1e-16, None, ALU.add)
                dve.drain()
                dve.reciprocal(rden, rden)
                dve.drain()
                for i in range(2):
                    last = dve.tensor_tensor(o_s[:, i, :].rearrange("p (h d) -> p h d", h=HEADS),
                                             acc_all[:, bass.ds(2 * g + i, 1), :, 0:HD].rearrange("p o h d -> p (o h) d"),
                                             rden[:, i, :].rearrange("p (h o) -> p h o", o=1).broadcast_to((P, HEADS, HD)), ALU.mult)
                last.then_inc(o_ready, 1)
                dve.wait_ge(y_ps, g + 1)
                dve.tensor_tensor(xs[:, t2, :].rearrange("p t d -> p (t d)"), xs[:, t2, :].rearrange("p t d -> p (t d)"),
                                  banks(1, 4), ALU.add).then_inc(x1_ready, 1)
            dve.drain()
            all_stats()
            dve.tensor_scalar(nrm[:, 0, :], meanvar[:, :, 1], 1e-5, None, ALU.add).then_inc(var2_ready, 1)
            dve.wait_ge(sd2_ready, 1)
            dve.reciprocal(nrm[:, 3, :], nrm[:, 1, :])
            dve.drain()
            with dve.Fori(0, NG) as g:
                for i in range(2):
                    t = bass.ds(2 * g + i, 1)
                    if i == 0:
                        dve.wait_ge(ht_ready, g + 1)
                    last = dve.tensor_scalar(h_s[:, i, :], xs[:, t, :].rearrange("p o d -> p (o d)"),
                                             meanvar[:, t, 0], nrm[:, 3, t], ALU.subtract, ALU.mult)
                last.then_inc(h_ready, 1)
            phase(dve, 3)

            dve.sem_inc(sim_free, 2)
            dve.sem_inc(mlp_added, 1)
            dve.sem_inc(comp_out, 16)
            with dve.Fori(0, NG) as g:
                dve.wait_ge(silu_ready, g + 1)
                dve.wait_ge(u_ps, g + 1)
                dve.tensor_tensor(a_t.rearrange("p k c -> p (k c)"), sg, banks(4, 2), ALU.mult).then_inc(at_ready, 1)
                for i in range(2):
                    sx, sy = sim[:, i, 0:HEADS, :], sim[:, i, HEADS:KEYP, :]
                    ey, rr, thr, ex, cl = parts(comp)
                    dve.drain()
                    dve.wait_ge(sim_ready, 2 * g + i + 3)
                    dve.memset(pace_dve[:], 0.0)
                    dve.drain()
                    for a in range(KEYP):
                        dve.max(s8[:, a, :], sim[:, i, a, :])
                    dve.drain()
                    for a in range(KEYP):
                        dve.max_index(i8[:, a, :], s8[:, a, :], sim[:, i, a, :])
                    gv = grid.rearrange("p (h a b) -> p h a b", h=HEADS, a=TOP)
                    for h in range(HEADS):
                        dve.tensor_tensor(gv[:, h, :, :],
                                          s8[:, h, :].rearrange("p (a o) -> p a o", o=1).broadcast_to((P, TOP, TOP)),
                                          s8[:, HEADS + h, :].rearrange("p (o b) -> p o b", o=1).broadcast_to((P, TOP, TOP)), ALU.add)
                    dve.tensor_tensor(e8, s8, s8[:, :, 0:1].broadcast_to((P, KEYP, TOP)), ALU.subtract)
                    dve.wait_ge(comp_out, 32 * g + 16 * i + 16)
                    dve.tensor_tensor(ey, sy, s8[:, HEADS:KEYP, 0:1].broadcast_to((P, HEADS, NK)), ALU.subtract)
                    dve.tensor_tensor(ex, sx[:, :, 0:NX], s8[:, 0:HEADS, 0:1].broadcast_to((P, HEADS, NX)), ALU.subtract)\
                        .then_inc(ex_in_ready, 1)
                    dve.drain()
                    dve.sem_inc(sim_free, 1)
                    dve.tensor_copy(i8f, i8)
                    for h in range(HEADS):
                        dve.max(g8[:, h, :], grid[:, h * 64:h * 64 + 64])
                    dve.drain()
                    for h in range(HEADS):
                        dve.match_replace(grid_r[:, h * 64:h * 64 + 64], g8[:, h, :], grid[:, h * 64:h * 64 + 64], -BIG)
                    dve.drain()
                    dve.tensor_tensor(sel, grid_r, grid, ALU.not_equal)
                    dve.drain()
                    dve.tensor_reduce(n_i, sel.rearrange("p (a b) -> p a b", b=TOP), AX.X, ALU.add)
                    dve.memset(rr, 0.0)
                    for j in range(TOP):
                        dve.drain()
                        dve.tensor_tensor(eq.rearrange("p (h n) -> p h n", h=HEADS),
                                          iota_row[:].rearrange("p (o n) -> p o n", o=1).broadcast_to((P, HEADS, NK)),
                                          i8f[:, HEADS:KEYP, j:j + 1].broadcast_to((P, HEADS, NK)), ALU.is_equal)
                        dve.drain()
                        rf = rr.rearrange("p h n -> p (h n)")
                        dve.scalar_tensor_tensor(rf, eq, float(TOP - j), rf, ALU.mult, ALU.add)
                    dve.drain()
                    for h in range(HEADS):
                        eqx = eq[:, 0:NX * TOP].rearrange("p (x a) -> p x a", a=TOP)
                        dve.tensor_tensor(eqx, iota_row[:, 0:NX].rearrange("p (x o) -> p x o", o=1).broadcast_to((P, NX, TOP)),
                                          i8f[:, h, :].rearrange("p (o a) -> p o a", o=1).broadcast_to((P, NX, TOP)), ALU.is_equal)
                        dve.drain()
                        dve.tensor_tensor(eqx, eqx, n_i[:, h * TOP:(h + 1) * TOP].rearrange("p (o a) -> p o a", o=1)
                                          .broadcast_to((P, NX, TOP)), ALU.mult)
                        dve.drain()
                        dve.tensor_reduce(thr[:, h, :], eqx, AX.X, ALU.add)
                        dve.drain()
                    dve.tensor_scalar(thr, thr, -1.0, float(TOP + 1), ALU.mult, ALU.add)
                    dve.wait_ge(ex_ready, 2 * g + i + 1)
                    for h in range(HEADS):
                        dve.tensor_tensor(wsel[:, h * 64:h * 64 + 64].rearrange("p (a b) -> p a b", a=TOP),
                                          e8[:, h, :].rearrange("p (a o) -> p a o", o=1).broadcast_to((P, TOP, TOP)),
                                          e8[:, HEADS + h, :].rearrange("p (o b) -> p o b", o=1).broadcast_to((P, TOP, TOP)), ALU.mult)
                    dve.drain()
                    dve.tensor_tensor(wsel, wsel, sel, ALU.mult)
                    dve.drain()
                    dve.tensor_reduce(r_i, wsel.rearrange("p (a b) -> p a b", b=TOP), AX.X, ALU.add)
                    dve.drain()
                    dve.tensor_reduce(z_h, r_i.rearrange("p (h a) -> p h a", a=TOP), AX.X, ALU.add)
                    dve.drain()
                    dve.reciprocal(rz, z_h)
                    dve.drain()
                    rzb = rz.rearrange("p (h o) -> p h o", o=1)
                    dve.tensor_tensor(ex, ex, rzb.broadcast_to((P, HEADS, NX)), ALU.mult)
                    rv = r_i.rearrange("p (h a) -> p h a", a=TOP)
                    dve.tensor_tensor(rv, rv, rzb.broadcast_to((P, HEADS, TOP)), ALU.mult)
                    nv = n_i.rearrange("p (h a) -> p h a", a=TOP)
                    dve.tensor_scalar(nv, i8f[:, 0:HEADS, :], float(NX), None, ALU.is_ge)
                    dve.drain()
                    dve.tensor_tensor(nv, nv, rv, ALU.mult)
                    dve.drain()
                    dve.tensor_reduce(cl, n_i, AX.X, ALU.add)
                    dve.drain()
                    dve.sem_inc(comp_ready, 1)
                dve.wait_ge(mlp_ps, g + 1)
                xv = xs[:, bass.ds(2 * g, 2), :].rearrange("p t d -> p (t d)")
                dve.tensor_tensor(xv, xv, banks(2, 4), ALU.add).then_inc(mlp_added, 1)
            phase(dve, 4)

            dve.sem_inc(cmp_free, 2)
            dve.sem_inc(yx_added, 1)
            dve.sem_inc(v_ready, 1)

            def dve_expert_weights(m, q):
                for i in range(2):
                    ey, rr, thr, ex, cl = parts(cmp_in[:, i, :])
                    for b in range(EB):
                        for h in range(HEADS):
                            if b == 0 and h == 0:
                                dve.wait_ge(cmp_in_s[i], 16 * m + 16)
                                dve.wait_ge(st_ready, m + 1)
                            k = EB * q + b
                            dve.scalar_tensor_tensor(s_tmp[:, b, h, :], rr[:, h, :], thr[:, h, k:k + 1], ey[:, h, :], ALU.is_ge, ALU.mult)
                    dve.drain()
                    for h in range(HEADS):
                        for b in range(EB):
                            k = EB * q + b
                            if h == 0:
                                dve.tensor_scalar(s_q[:, i, b, :], s_tmp[:, b, h, :], ex[:, h, k:k + 1], None, ALU.mult)
                            else:
                                dve.scalar_tensor_tensor(s_q[:, i, b, :], s_tmp[:, b, h, :], ex[:, h, k:k + 1], s_q[:, i, b, :],
                                                         ALU.mult, ALU.add)
                        dve.drain()
                    if q == QE - 1:
                        dve.tensor_tensor(s_q[:, i, EB - 1, NK - 1:NK], s_q[:, i, EB - 1, NK - 1:NK], cl, ALU.add)
                        dve.drain()
                    dve.sem_inc(cmp_free, 1)
                dve.sem_inc(s_ready, 1)

            def dve_weigh_experts(m_1):
                dve.wait_ge(st_ready, m_1 + 1)
                dve.wait_ge(sd_act, m_1 + 1)
                dve.tensor_tensor(v_t.rearrange("p b c -> p (b c)"), sd_t.rearrange("p b c -> p (b c)"),
                                  s_t.rearrange("p b c -> p (b c)"), ALU.mult).then_inc(v_ready, 1)

            def dve_add_experts(m_1, g):
                dve.wait_ge(yx_ps, m_1)
                xv = xs[:, bass.ds(2 * g, 2), :].rearrange("p t d -> p (t d)")
                dve.tensor_tensor(xv, xv, banks(4, 4), ALU.add).then_inc(yx_added, 1)
                dve.drain()

            def dve_experts(m, q, g, before):
                dve_weigh_experts(m)
                dve_expert_weights(m, q)
                dve_add_experts(m, before)

            def dve_experts_last(before):
                dve_weigh_experts(NG * QE)
                dve_add_experts(NG * QE, before)

            run_experts(dve, lambda m, q, g: dve_expert_weights(m, q), dve_experts, dve_experts_last)

        @block.tensor
        def _(pe):
            pe.wait_ge(const_ready, 11)
            pe.wait_ge(wdn_scaled, 1)
            with pe.Fori(0, NG) as g:
                pe.wait_ge(xn_ready, g + 1)
                for k in range(KD):
                    for i in range(2):
                        a = k * GT + i * P
                        last = pe.transpose(banks(0, 4)[:, a:a + P], xn[:, i, k * P:(k + 1) * P], ident[:])
                last.then_inc(xnt_ps, 1)
                pe.wait_ge(xnt_ready, g + 2)
                for j in range(KH):
                    for k in range(KD):
                        last = pe.matmul(banks(4)[:, j * GT:(j + 1) * GT], wdn_s[:, k, j * P:(j + 1) * P], xnt[:, k, :],
                                         start=(k == 0), stop=(k == KD - 1))
                last.then_inc(zt_ps, 1)
                pe.wait_ge(zt_ready, g + 1)
                for i in range(2):
                    for k in range(KH):
                        last = pe.matmul(banks(5 + i), zt[:, k, i * P:(i + 1) * P], wlr_s[:, k, :],
                                         start=(k == 0), stop=(k == KH - 1))
                last.then_inc(xlr_ps, 1)
            pe.wait_ge(bnd_ready, 1)
            pe.transpose(ps[0:2 * NT, 7, 0:P], bnd_p, ident[:]).then_inc(bnd_ps, 1)
            pe.wait_ge(bnd_ready, 2)
            pe.transpose(ps[0:1, 7, P:P + 2 * NT], bnd_t[0:2 * NT, 0:1], ident[0:2 * NT, 0:2 * NT]).then_inc(bnd_ps, 1)
            pe.wait_ge(tab_ready, 1)
            phase(pe, 1)

            pe.wait_ge(attb_in, 16 * HEADS)

            def rows_of(m, b):
                return m.rearrange("p (e t) -> p t e", t=T)[:, b * HT:(b + 1) * HT, :]

            def pe_destinations(par, v):
                w = window_of(pe, v)
                for b in range(2):
                    if b == 0:
                        pe.wait_ge(ohd_ready, v + 1)
                    if not isinstance(v, int):
                        pe.wait_ge(lrelu_ready[b], v)
                    for k in range(KH):
                        for s in range(3):
                            pe.matmul(banks(2 * b + k).rearrange("p (t e) -> p t e", t=HT),
                                      xr3[:, bass.ds(w, 1), s, k * P:(k + 1) * P].rearrange("p o n -> p (o n)"),
                                      rows_of(oh_d[par], b), start=(s == 0), stop=False, skip_group_check=True)

            def pe_sources(par, v, n, b):
                pe.wait_ge(g_in[par][b], 16 * HT * n + 16 * HT)
                for k in range(KH):
                    for t in range(HT):
                        last = pe.matmul(ps[:, 2 * b + k, t * P:(t + 1) * P], gath[par][:, b * HT + t, k * P:(k + 1) * P], ident[:],
                                         start=False, stop=(t == HT - 1), skip_group_check=True)
                last.then_inc(msg_ps[b], 1)

            def pe_scores(v):
                for b in range(2):
                    if b == 0 and not isinstance(v, int):
                        pe.wait_ge(bc_copied, 8 * v)
                    pe.wait_ge(lrelu_ready[b], v + 1)
                    for k in range(KH):
                        last = pe.matmul(ps[0:HEADS, 4 + b, :], att_b[:, k, :], lrelu_t[:, b, k * HT * P:(k + 1) * HT * P],
                                         start=(k == 0), stop=(k == KH - 1))
                    last.then_inc(e_ps[b], 1)

            def pe_score_rows(v):
                pe.wait_ge(mask_ready, v + 1)
                for k in range(2 * HEADS):
                    b, h = k // HEADS, k % HEADS
                    if k == 0:
                        pe.wait_ge(e_copied[0], v + 1)
                    if k == 2:
                        pe.wait_ge(e_copied[1], v + 1)
                    if k >= 3:
                        pe.wait_ge(bc_copied, 8 * v + k - 2)
                    o = banks(ROW_BANK[k % 3])
                    pe.matmul(o.rearrange("p (t e) -> p t e", t=HT), ident_b[:], rows_of(mask, b),
                              start=True, stop=False, skip_group_check=True)
                    pe.matmul(o, ident_b[0:HEADS, h:h + 1].broadcast_to((HEADS, P)), e_row_b[0:HEADS, b, :],
                              start=False, stop=True, skip_group_check=True).then_inc(bc_ps, 1)

            def pe_exponents(par, v):
                pe.wait_ge(mw_ready, v + 1)
                for t in range(T):
                    o = ps[:, 7, SUMS + t * HEADS:SUMS + (t + 1) * HEADS]
                    pe.matmul(o, e_row[0:HEADS, t // HT, (t % HT) * P:(t % HT + 1) * P], ident[0:HEADS, 0:HEADS],
                              start=True, stop=False, skip_group_check=True)
                    last = pe.matmul(o, oh_d[par].rearrange("p (e t) -> p t e", t=T)[:, t, :], m_neg,
                                     start=False, stop=True, skip_group_check=True)
                last.then_inc(z_ps, 1)

            def pe_sums(v, b):
                pe.wait_ge(wg_ready[b], v + 1)
                for t in range(b * HT, (b + 1) * HT):
                    last = pe.matmul(ps[:, 7, 0:SUMS], oh_e[:, t, :], wgt[:, t, :], start=(t == 0), stop=(t == T - 1))
                if b == 1:
                    last.then_inc(sc_ps, 1)

            def pe_front(par, v, n):
                pe_destinations(par, v)
                pe_sources(par, v, n, 0)
                pe_sources(par, v, n, 1)
                pe_scores(v)
                pe_score_rows(v)

            def pe_both(par, v, n, before):
                pe_destinations(par, v)
                pe_exponents(1 - par, before)
                pe_sources(par, v, n, 0)
                pe_sources(par, v, n, 1)
                pe_sums(before, 0)
                pe_sums(before, 1)
                pe_scores(v)
                pe_score_rows(v)

            def pe_last(v):
                pe_exponents(1, v)
                pe_sums(v, 0)
                pe_sums(v, 1)

            run_visits(pe, pe_front, pe_both, pe_last)
            phase(pe, 2)
            pe.wait_ge(fw_in, 7 * 16)
            with pe.Fori(0, NG) as g:
                pe.wait_ge(o_ready, g + 1)
                for k in range(KH):
                    for i in range(2):
                        a = k * GT + i * P
                        last = pe.transpose(banks(0)[:, a:a + P], o_s[:, i, k * P:(k + 1) * P], ident[:])
                last.then_inc(ot_ps, 1)
                pe.wait_ge(ot_ready, g + 1)
                for i in range(2):
                    for n in range(2):
                        for k in range(KH):
                            last = pe.matmul(banks(1 + 2 * i + n), o_t[:, k, i * P:(i + 1) * P],
                                             wup_s[:, k, n * 512:(n + 1) * 512], start=(k == 0), stop=(k == KH - 1))
                last.then_inc(y_ps, 1)
            pe.wait_ge(x1_ready, NG)
            pe.sem_inc(ht_ready, 1)
            with pe.Fori(0, NG) as g:
                pe.wait_ge(h_ready, g + 1)
                for k in range(KD):
                    for i in range(2):
                        a = k * GT + i * P
                        last = pe.transpose(banks(0, 4)[:, a:a + P], h_s[:, i, k * P:(k + 1) * P], ident[:])
                last.then_inc(ht_ps, 1)
            phase(pe, 3)
            with pe.Fori(0, NG) as g:
                hg = ht[:, :, bass.ds(g * GT, GT)]

                def turned(a, w, m):
                    for j in range(m):
                        for k in range(KD):
                            last = pe.matmul(banks(a, 2)[:, j * GT:(j + 1) * GT], w[:, k, j * P:(j + 1) * P], hg[:, k, :],
                                             start=(k == 0), stop=(k == KD - 1))
                    return last

                pe.wait_ge(sim_ready, 2 * g + 2)
                turned(0, wq_s, HEADS).then_inc(q_ps, 1)
                pe.wait_ge(mlp_added, g + 1)
                turned(2, wg_s, KI).then_inc(g_ps, 1)
                turned(4, wu_s, KI).then_inc(u_ps, 1)
                for i in range(2):
                    if i == 0:
                        pe.wait_ge(qt_ready, g + 2)
                    for j in range(HEADS):
                        last = pe.matmul(banks(6 * (1 - i), 2)[:, j * 2 * NK:(j + 1) * 2 * NK], qt[:, j, i * P:(i + 1) * P],
                                         keys_s[:, j, :, :].rearrange("p a n -> p (a n)"), start=True, stop=True)
                    last.then_inc(sim_ps, 1)
                pe.wait_ge(at_ready, g + 1)
                for i in range(2):
                    for n in range(2):
                        for k in range(KI):
                            last = pe.matmul(banks(2 + 2 * i + n), a_t[:, k, i * P:(i + 1) * P],
                                             wd_s[:, k, n * 512:(n + 1) * 512], start=(k == 0), stop=(k == KI - 1))
                last.then_inc(mlp_ps, 1)
            phase(pe, 4)

            def pe_down(m, q, g):
                dn = slot[2 * (q % 2)][:, :].rearrange("p (k n) -> p k n", k=KD)
                hg = ht[:, :, bass.ds(g * GT, GT)]
                pe.wait_ge(sd_act, m + 1)
                for j in range(EB):
                    for k in range(KD):
                        last = pe.matmul(banks(2, 2)[:, j * GT:(j + 1) * GT], dn[:, k, j * P:(j + 1) * P], hg[:, k, :],
                                         start=(k == 0), stop=(k == KD - 1))
                last.then_inc(d_ps, 1)

            def pe_turn_weights(m):
                pe.wait_ge(s_ready, m + 1)
                for b in range(EB):
                    for i in range(2):
                        a = b * GT + i * P
                        last = pe.transpose(banks(0, 2)[:, a:a + P], s_q[:, i, b, :], ident[:])
                last.then_inc(st_ps, 1)

            def pe_up(m_1, q):
                uw = slot[2 * (q % 2) + 1][:, :].rearrange("p (k n) -> p k n", k=EB)
                pe.wait_ge(v_ready, m_1 + 1)
                pe.wait_ge(yx_added, m_1)
                for i in range(2):
                    for n in range(2):
                        for b in range(EB):
                            last = pe.matmul(banks(4 + 2 * i + n), v_t[:, b, i * P:(i + 1) * P],
                                             uw[:, b, n * 512:(n + 1) * 512], start=(b == 0), stop=(b == EB - 1))
                last.then_inc(yx_ps, 1)

            def pe_experts_first(m, q, g):
                pe.wait_ge(dw_in[0], 32)
                pe_down(m, q, g)
                pe_turn_weights(m)

            def pe_experts(m, q, g, before):
                if isinstance(g, int):
                    pe.wait_ge(dw_in[q % 2], 32 * (q // 2 + 1))
                pe_down(m, q, g)
                pe_up(m, q - 1 if isinstance(g, int) else q)
                pe_turn_weights(m)

            run_experts(pe, pe_experts_first, pe_experts, lambda before: pe_up(NG * QE, QE - 1))


def kernel(x, src, dst, L0_gnn_rms_w, L0_gnn_W_down, L0_gnn_Wl, L0_gnn_Wr, L0_gnn_att, L0_gnn_W_up, L0_ffn_Wq,
           L0_ffn_keys, L0_ffn_down_embed, L0_ffn_up_embed, L0_ffn_Wg, L0_ffn_Wu, L0_ffn_Wd):
    import numpy as np
    import concourse.bacc as bacc
    from concourse import mybir
    from concourse.bass_utils import run_bass_kernel_spmd

    chunk = 1024
    pad = -len(src) % chunk
    arrays = {
        "x": x,
        "src": np.pad(src, (0, pad)),
        "dst": np.pad(dst, (0, pad), constant_values=-1),
        "rms_w": L0_gnn_rms_w.reshape(-1, 128).T,
        "w_down": L0_gnn_W_down,
        "w_l": L0_gnn_Wl,
        "w_r": L0_gnn_Wr,
        "att": L0_gnn_att,
        "w_up": L0_gnn_W_up,
        "wq_t": L0_ffn_Wq.T,
        "keys_t": L0_ffn_keys.transpose(3, 2, 0, 1),
        "down_t": L0_ffn_down_embed.T,
        "up": L0_ffn_up_embed,
        "wg_t": L0_ffn_Wg.T,
        "wu_t": L0_ffn_Wu.T,
        "wd_t": L0_ffn_Wd.T,
    }
    arrays = {f"in_{k}": np.ascontiguousarray(v) for k, v in arrays.items()}
    nc = bacc.Bacc("TRN2", target_bir_lowering=False, num_devices=1)
    args = [nc.dram_tensor(k, v.shape, mybir.dt.from_np(v.dtype), kind="ExternalInput").ap() for k, v in arrays.items()]
    out = nc.dram_tensor("out", x.shape, mybir.dt.float32, kind="ExternalOutput").ap()
    gnn_then_peer_ffn(nc, *args, out)
    r = run_bass_kernel_spmd(nc, [arrays], core_ids=[0])
    return r.results[0]["out"]
```

```python
from contextlib import ExitStack

import concourse.bass as bass
from concourse import mybir

F32 = mybir.dt.float32
BF16 = mybir.dt.bfloat16
I32 = mybir.dt.int32
U32 = mybir.dt.uint32
ALU = mybir.AluOpType
ACT = mybir.ActivationFunctionType
AX = mybir.AxisListType
P = 128
BIG = 3.0e38


def gnn_then_peer_ffn(nc, x, src, dst, dst_cols, rms_w, w_down, w_l, w_r, att, w_up, wq_t, keys_t, down_t, up, wg_t, wu_t,
                      wd_t, out):
    N, D = x.shape
    HID = w_down.shape[1]
    HEADS, HD = att.shape
    NT = -(-N // P)
    LAST = N - (NT - 1) * P
    KD = D // P
    KH = HID // P
    T = 8
    HT = T // 2
    CH = T * P
    NCH = src.shape[0] // CH
    MAXV = NT * NCH + 2
    SLOT = HD + 1
    SUMS = HEADS * SLOT
    EH = T * HEADS
    NG = NT // 2
    GT = 2 * P
    QH = wq_t.shape[1] // (2 * HEADS)
    NK = keys_t.shape[3]
    TOP = 8
    INTER = wg_t.shape[1]
    KI = INTER // P
    NE = up.shape[0]
    NX = NE // NK
    QE = 4
    EB = NE // P // QE
    KEYP = 2 * HEADS
    assert NCH <= P and KD * P == D and NG * 2 == NT and HEADS * HD == HID and NK == P and QH * 2 == P

    with ExitStack() as ctx:
        def sb(name, shape, dt=F32):
            return ctx.enter_context(nc.sbuf_tensor(name, shape, dt))

        def sem(name):
            return ctx.enter_context(nc.semaphore(name))

        xs = sb("xs", [P, NT, D])
        slot4 = sb("slot4", [P, (NT + 1) * HEADS * SLOT + KH * D])
        acc_all = slot4[:, KH * D:].rearrange("p (t h s) -> p t h s", t=NT + 1, h=HEADS)
        wup_s = slot4[:, 0:KH * D].rearrange("p (k n) -> p k n", k=KH)
        ident = sb("ident", [P, P])
        ident_b = sb("ident_b", [P, P], BF16)
        iota_row = sb("iota_row", [P, P])
        iota_row_b = sb("iota_row_b", [P, P], BF16)
        iota_part = sb("iota_part", [P, 1])
        win_base = sb("win_base", [P, NT + 1])
        win_node = sb("win_node", [P, NT + 1])
        stats = sb("stats", [P, NT, 2, 6])
        meanvar = sb("meanvar", [P, NT, 2])
        nrm = sb("nrm", [P, 4, NT])
        pace_act = sb("pace_act", [P, 1])
        pace_dve = sb("pace_dve", [P, 1])
        pace_pool = sb("pace_pool", [P, 4], I32)
        zero_pool = sb("zero_pool", [P, 1], I32)
        WS = KD * INTER
        slot = [sb("slot0", [P, WS]), sb("slot1", [P, WS])]
        keys_s = sb("keys_s", [P, HEADS, 2, NK])
        wq_s = slot[0][:].rearrange("p (k n) -> p k n", k=KD)
        wg_s = slot[1][:].rearrange("p (k n) -> p k n", k=KD)
        AR = 27 * 1024
        arena = sb("arena", [P, AR])
        at = [0]

        def carve(n, dt=F32):
            w = n if dt != BF16 else n // 2
            v = arena[:, at[0]:at[0] + w]
            at[0] += w
            assert at[0] <= AR, at[0]
            return v if dt == F32 else v.bitcast(dt)

        xr3 = carve((NT + 1) * 3 * HID, BF16).rearrange("p (t s n) -> p t s n", t=NT + 1, s=3)
        att_b = carve(KH * HEADS).rearrange("p (k h) -> p k h", k=KH)
        att_w = carve(KH * T * EH).rearrange("p (k t j) -> p k t j", k=KH, t=T)
        dcol = carve(NCH * T)
        m_all = carve((NT + 1) * HEADS).rearrange("p (t h) -> p t h", t=NT + 1)
        visits = carve(2 * MAXV, I32).rearrange("p (a v) -> p a v", a=2)
        n_pairs = carve(2, I32)
        g_at = at[0]
        xl = carve(NT * HID).rearrange("p (t n) -> p t n", t=NT)
        xr = carve(NT * HID).rearrange("p (t n) -> p t n", t=NT)
        wdn_s = carve(KD * HID).rearrange("p (k n) -> p k n", k=KD)
        wlr_s = carve(KH * 2 * HID).rearrange("p (k n) -> p k n", k=KH)
        zt = carve(KH * GT).rearrange("p (k c) -> p k c", k=KH)
        self_m = carve(2 * HID).rearrange("p (t n) -> p t n", t=2)
        rms_s = carve(KD)
        att_s = carve(HID)
        dst_i = carve(NCH * T, I32)
        m_self = carve(NT * HEADS, BF16)
        e_self = carve(NT * HEADS)
        p_self = carve(NT * HEADS)
        ext_p = carve(2 * NCH)
        ext_c = carve(4)
        bnd_p = carve(2 * NT)
        bnd_t = carve(4)
        first_c = carve(2)
        one_c = carve(1)
        bnd_r = carve(5 * NT).rearrange("p (a w) -> p a w", a=5)
        visits_n = carve(MAXV)
        assert WS >= 4 * D
        xn = slot[1][:, 0:2 * D].rearrange("p (i d) -> p i d", i=2)
        xnt = slot[1][:, 2 * D:4 * D].rearrange("p (k c) -> p k c", k=KD)
        visits_f = slot[0][:, 0:3 * MAXV].rearrange("p (a v) -> p a v", a=3)
        xr_rest = slot[0][:, 3 * MAXV:3 * MAXV + 2 * HID].rearrange("p (t n) -> p t n", t=2)
        at[0] = g_at
        gath = [carve(T * HID).rearrange("p (t n) -> p t n", t=T) for _ in range(2)]
        wgt = carve(T * HEADS * SLOT).rearrange("p (t n) -> p t n", t=T)
        lrelu_t = carve(T * HID).rearrange("p (b n) -> p b n", b=2)
        oh_e = [carve(T * P).rearrange("p (t n) -> p t n", t=T) for _ in range(2)]
        oh_d = [carve(CH, BF16) for _ in range(2)]
        mask = carve(CH, BF16)
        xr_w = [carve(3 * HID, BF16).rearrange("p (s n) -> p s n", s=3) for _ in range(2)]
        drow = carve(CH, I32)
        idx = [carve(T, I32) for _ in range(2)]
        e_row = carve(P)
        e_row_b = carve(P, BF16)
        score_r = carve(2 * HEADS * HT * P, BF16).rearrange("p (b n) -> p b n", b=2)
        fold = carve(HEADS * HT * P, BF16).rearrange("p (h n) -> p h n", h=HEADS)
        dcol_c = [carve(T) for _ in range(2)]
        z_e = carve(T * HEADS)
        cmax = carve(HEADS)
        m_neg = carve(HEADS, BF16)
        m_n = carve(HEADS)
        m_d = carve(HEADS)
        m_s = carve(HEADS)
        at[0] = 0
        ht = carve(KD * NT * P).rearrange("p (k c) -> p k c", k=KD)
        slot += [carve(WS), carve(WS)]
        wu_s = slot[2].rearrange("p (k n) -> p k n", k=KD)
        wd_s = slot[3].rearrange("p (k n) -> p k n", k=KI)
        assert KH * D + (NT + 1) * HEADS * SLOT >= WS
        slot += [slot4[:, 0:WS]]
        dn_s = [slot[a][:, 0:WS].rearrange("p (k n) -> p k n", k=KD) for a in (4, 1, 3, 0)]
        up_s = [slot[a][:, 0:WS].rearrange("p (k n) -> p k n", k=EB) for a in (0, 2, 4, 1)]
        f_at = at[0]
        o_s = carve(2 * HID).rearrange("p (i n) -> p i n", i=2)
        o_t = carve(KH * GT).rearrange("p (k c) -> p k c", k=KH)
        rden = carve(2 * HEADS).rearrange("p (i h) -> p i h", i=2)
        stats_g = carve(2 * 2 * 6).rearrange("p (i a s) -> p i a s", i=2, a=2)
        meanvar_g = carve(4).rearrange("p (i m) -> p i m", i=2)
        var_g = carve(2)
        rstd_g = carve(2)
        h_s = carve(2 * D).rearrange("p (i d) -> p i d", i=2)
        at[0] = f_at
        qt = carve(HEADS * GT).rearrange("p (j c) -> p j c", j=HEADS)
        sim = carve(2 * KEYP * NK).rearrange("p (i a n) -> p i a n", i=2, a=KEYP)
        sg = carve(KI * GT)
        a_t = carve(KI * GT).rearrange("p (k c) -> p k c", k=KI)
        COMP = 2 * HEADS * NK + 2 * HEADS * NX + 1
        comp = carve(COMP)
        s8 = carve(KEYP * TOP).rearrange("p (a n) -> p a n", a=KEYP)
        i8 = carve(KEYP * TOP, U32).rearrange("p (a n) -> p a n", a=KEYP)
        i8f = carve(KEYP * TOP).rearrange("p (a n) -> p a n", a=KEYP)
        e8 = carve(KEYP * TOP).rearrange("p (a n) -> p a n", a=KEYP)
        grid = carve(HEADS * TOP * TOP)
        grid_r = slot4[:, WS:WS + HEADS * TOP * TOP]
        at_first = slot4[:, WS + HEADS * TOP * TOP:WS + HEADS * TOP * (TOP + NX)].rearrange("p (h x a) -> p h x a", h=HEADS, x=NX)
        sel = carve(HEADS * TOP * TOP)
        wsel = grid_r
        g8 = carve(HEADS * TOP).rearrange("p (h n) -> p h n", h=HEADS)
        n_i = carve(HEADS * TOP)
        r_i = carve(HEADS * TOP)
        z_h = carve(HEADS)
        rz = carve(HEADS)
        ranks = carve(TOP * HEADS * NK, BF16).rearrange("p (j h n) -> p j h n", j=TOP, h=HEADS)
        at[0] = f_at
        cmp_in = carve(2 * COMP).rearrange("p (i n) -> p i n", i=2)
        s_q = carve(2 * EB * NK).rearrange("p (i b n) -> p i b n", i=2, b=EB)
        s_tmp = carve(EB * HEADS * NK).rearrange("p (b h n) -> p b h n", b=EB, h=HEADS)
        s_t = carve(EB * GT).rearrange("p (b c) -> p b c", b=EB)
        sd_t = carve(EB * GT).rearrange("p (b c) -> p b c", b=EB)
        v_t = carve(EB * GT).rearrange("p (b c) -> p b c", b=EB)

        def parts(c):
            a, b = HEADS * NK, HEADS * NX
            return (c[:, 0:a].rearrange("p (h n) -> p h n", h=HEADS),
                    c[:, a:2 * a].rearrange("p (h n) -> p h n", h=HEADS),
                    c[:, 2 * a:2 * a + b].rearrange("p (h n) -> p h n", h=HEADS),
                    c[:, 2 * a + b:2 * a + 2 * b].rearrange("p (h n) -> p h n", h=HEADS),
                    c[:, COMP - 1:COMP])

        ps = ctx.enter_context(nc.psum_tensor("ps", [P, 8, 512], F32))

        def banks(a, n=1):
            return ps[:, a:a + n, :].rearrange("p b n -> p (b n)")

        ROW_BANK = (4, 6, 5)
        xl_dram = nc.dram_tensor("xl_rows", (NT * P, HID), F32, kind="Internal").ap()
        comp_dram = nc.dram_tensor("comp_rows", (NT, P, COMP), F32, kind="Internal").ap()

        x_pad0 = sem("x_pad0")
        x_in = [sem(f"x_in_{g}") for g in range(NG)]
        dst_in = sem("dst_in")
        x_tail = sem("x_tail")
        gw_in = sem("gw_in")
        ew_in = sem("ew_in")
        const_ready = sem("const_ready")
        wdn_scaled = sem("wdn_scaled")
        var_ready = sem("var_ready")
        sd_ready = sem("sd_ready")
        xn_ready = sem("xn_ready")
        xnt_ps = sem("xnt_ps")
        xnt_ready = sem("xnt_ready")
        zt_ps = sem("zt_ps")
        zt_ready = sem("zt_ready")
        xlr_ps = sem("xlr_ps")
        xl_ready = sem("xl_ready")
        attb_zero = sem("attb_zero")
        attb_in = sem("attb_in")
        attw_ready = sem("attw_ready")
        xl_out = sem("xl_out")
        bnd_ready = sem("bnd_ready")
        bnd_ps = sem("bnd_ps")
        sz_ready = sem("sz_ready")
        sp_ready = sem("sp_ready")
        tab_ready = sem("tab_ready")
        tab_ps = sem("tab_ps")
        drow_in = sem("drow_in")
        idx_in = [sem("idx_in_0"), sem("idx_in_1")]
        drow_free = sem("drow_free")
        idx_free = sem("idx_free")
        idx_seen = sem("idx_seen")
        g_in = [[sem("g_in_0a"), sem("g_in_0b")], [sem("g_in_1a"), sem("g_in_1b")]]
        g_free = [sem("g_free_a"), sem("g_free_b")]
        ohd_ready = sem("ohd_ready")
        mask_ready = sem("mask_ready")
        mw_ready = sem("mw_ready")
        msg_ps = [sem("msg_ps_a"), sem("msg_ps_b")]
        scaled_ready = [sem("scaled_ready_a"), sem("scaled_ready_b")]
        lrelu_ready = [sem("lrelu_ready_a"), sem("lrelu_ready_b")]
        e_ps = sem("e_ps")
        e_copied = sem("e_copied")
        bc_ps = sem("bc_ps")
        bc_copied = sem("bc_copied")
        fold_done = sem("fold_done")
        m_ready = sem("m_ready")
        z_ps = sem("z_ps")
        ms_ready = sem("ms_ready")
        z_ready = sem("z_ready")
        p_ready = sem("p_ready")
        wg_ready = [sem("wg_ready_a"), sem("wg_ready_b")]
        sc_ps = sem("sc_ps")
        phase_done = sem("phase_done")
        fw_in = sem("fw_in")
        wup_in = sem("wup_in")
        fw2_in = sem("fw2_in")
        keys_zero = sem("keys_zero")
        o_ready = sem("o_ready")
        ot_ps = sem("ot_ps")
        ot_ready = sem("ot_ready")
        y_ps = sem("y_ps")
        x1_ready = sem("x1_ready")
        var2_ready = sem("var2_ready")
        sd2_ready = sem("sd2_ready")
        h_ready = sem("h_ready")
        ht_ps = sem("ht_ps")
        ht_ready = sem("ht_ready")
        q_ps = sem("q_ps")
        g_ps = sem("g_ps")
        u_ps = sem("u_ps")
        qt_ready = sem("qt_ready")
        silu_ready = sem("silu_ready")
        at_ready = sem("at_ready")
        sim_ps = sem("sim_ps")
        sim_ready = sem("sim_ready")
        sim_free = sem("sim_free")
        mlp_ps = sem("mlp_ps")
        mlp_added = sem("mlp_added")
        ex_in_ready = sem("ex_in_ready")
        ex_ready = sem("ex_ready")
        comp_ready = sem("comp_ready")
        comp_out = sem("comp_out")
        cmp_in_s = [sem("cmp_in_0"), sem("cmp_in_1")]
        cmp_free = sem("cmp_free")
        dn_in = [sem(f"dn_in_{q}") for q in range(QE)]
        up_in = [sem(f"up_in_{q}") for q in range(QE)]
        s_ready = sem("s_ready")
        st_ps = sem("st_ps")
        st_ready = sem("st_ready")
        d_ps = sem("d_ps")
        sd_act = sem("sd_act")
        v_ready = sem("v_ready")
        yx_ps = sem("yx_ps")
        yx_added = sem("yx_added")
        out_done = sem("out_done")

        block = ctx.enter_context(nc.Block())

        def phase(eng, n):
            eng.drain()
            eng.sem_inc(phase_done, 1)
            eng.wait_ge(phase_done, 5 * n)

        class Visit:
            def __init__(self, par, v, n):
                self.par, self.v, self.n = par, v, n
                self.w = self.c = None

            def load_window(self, eng):
                self.w = eng.value_load(visits[0:1, 0, bass.ds(self.v, 1)], min_val=0, max_val=NT)

            def load_chunk(self, eng):
                self.c = eng.value_load(visits[0:1, 1, bass.ds(self.v, 1)], min_val=0, max_val=NCH - 1)

        def run_visits(eng, front, both, last):
            later = eng.value_load(n_pairs[0:1, 1:2], min_val=NT // 2 - 1, max_val=MAXV // 2 - 2)
            front(Visit(0, 0, 0), Visit(1, 1, 0))
            with eng.Fori(0, later) as i:
                a, b, c = Visit(0, 2 * i, i), Visit(1, 2 * i + 1, i), Visit(0, 2 * i + 2, i + 1)
                both(b, a, c)
                both(c, b, Visit(1, 2 * i + 3, i + 1))
            a, b = Visit(0, 2 * later, later), Visit(1, 2 * later + 1, later)
            both(b, a, None)
            last(b)

        def run_experts(eng, first, both, last, started=0):
            for q in range(QE):
                if q == 0:
                    first(0, 0, 0)
                else:
                    both(NG * q, q, 0, NG - 1)
                k = started if q == 0 else 0
                with eng.Fori(0, NG - 1 - k) as g:
                    both(g + (NG * q + 1 + k), q, g + (1 + k), g + k if k else g)
            last(NG - 1)

        @block.sync
        def _(sp):
            sp.dma_start(dst_i.rearrange("p (c t) -> p c t", t=T), dst_cols.rearrange("(c p t) -> p c t", p=P, t=T)).then_inc(dst_in, 16)
            def load_x(g):
                n = 2 if g < NG - 1 else 1
                sp.dma_start(xs[:, 2 * g:2 * g + n, :], x[2 * g * P:(2 * g + n) * P, :].rearrange("(t p) d -> p t d", p=P))\
                    .then_inc(x_in[g], 16)

            load_x(0)
            sp.dma_start(wdn_s, w_down.rearrange("(k p) n -> p k n", p=P)).then_inc(gw_in, 16)
            sp.dma_start(rms_s, rms_w).then_inc(gw_in, 16)
            sp.dma_start(wlr_s[:, :, 0:HID], w_l.rearrange("(k p) n -> p k n", p=P)).then_inc(gw_in, 16)
            sp.dma_start(wlr_s[:, :, HID:2 * HID], w_r.rearrange("(k p) n -> p k n", p=P)).then_inc(gw_in, 16)
            for g in range(1, NG):
                load_x(g)
            sp.wait_ge(x_pad0, 1)
            sp.dma_start(xs[0:LAST, NT - 1, :], x[(NT - 1) * P:N, :]).then_inc(x_tail, 16)
            sp.dma_start(att_s, att.rearrange("(o h) d -> o (h d)", o=1).broadcast_to((P, HID))).then_inc(ew_in, 16)
            sp.wait_ge(attb_zero, 1)
            with nc.allow_non_contiguous_dma(reason="256 numbers once"):
                for h in range(HEADS):
                    r = (h % 2) * HD
                    sp.dma_start(att_b[r:r + HD, h // 2, h:h + 1], att[h:h + 1, :].rearrange("o d -> d o")).then_inc(attb_in, 16)
            sp.dma_start(wup_s, w_up.rearrange("(k p) n -> p k n", p=P)).then_inc(wup_in, 16)
            sp.wait_ge(keys_zero, 1)
            for r in range(2):
                for a in range(2):
                    sp.dma_start(keys_s[QH * r:QH * r + QH, 2 * a:2 * a + 2, r, :],
                                 keys_t[:, a, r::2, :]).then_inc(fw_in, 16)
            sp.wait_ge(xl_ready, 1)
            sp.dma_start(xl_dram.rearrange("(t p) n -> p t n", p=P), xl).then_inc(xl_out, 16)
            phase(sp, 1)

            def sp_front(at):
                at.load_chunk(sp)
                v, c, par = at.v, at.c, at.par
                sp.wait_ge(idx_seen, v + 1)
                sp.wait_ge(idx_free, v + 1)
                sp.dma_start(idx[par], src[bass.ds(c * CH, CH)].rearrange("(p t) -> p t", t=T)).then_inc(idx_in[par], 16)
                sp.wait_ge(drow_free, v + 1)
                sp.dma_start(drow, dst[bass.ds(c * CH, CH)].rearrange("(o n) -> o n", o=1).broadcast_to((P, CH)))\
                    .then_inc(drow_in, 16)

            run_visits(sp, lambda at, after: sp_front(at), lambda at, before, after: sp_front(at), lambda at: None)
            phase(sp, 2)
            sp.dma_start(wq_s, wq_t.rearrange("(k p) n -> p k n", p=P)).then_inc(fw2_in, 16)
            sp.dma_start(wg_s, wg_t.rearrange("(k p) n -> p k n", p=P)).then_inc(fw2_in, 16)
            sp.dma_start(wu_s, wu_t.rearrange("(k p) n -> p k n", p=P)).then_inc(fw2_in, 16)
            sp.dma_start(wd_s, wd_t.rearrange("(k p) n -> p k n", p=P)).then_inc(fw2_in, 16)
            sp.wait_ge(fw_in, 4 * 16)
            sp.wait_ge(fw2_in, 4 * 16)
            phase(sp, 3)
            with sp.Fori(0, NT) as t:
                sp.wait_ge(comp_ready, t + 1)
                sp.dma_start(comp_dram[bass.ds(t, 1), :, :].rearrange("o p n -> p (o n)"), comp).then_inc(comp_out, 16)
            sp.wait_ge(comp_out, 16 * NT + 16)
            phase(sp, 4)

            for q in range(QE):
                with sp.Fori(0, NG) as g:
                    for i in range(2):
                        sp.wait_ge(cmp_free, 2 * NG * q + 2 * g + i + 1)
                        sp.dma_start(cmp_in[:, i, :], comp_dram[bass.ds(2 * g + i, 1), :, :].rearrange("o p n -> p (o n)"))\
                            .then_inc(cmp_in_s[i], 16)
            for g in range(NG):
                n = 2 if g < NG - 1 else 1
                sp.wait_ge(yx_added, NG * (QE - 1) + g + 2)
                sp.dma_start(out[2 * g * P:(2 * g + n) * P, :].rearrange("(t p) d -> p t d", p=P), xs[:, 2 * g:2 * g + n, :])\
                    .then_inc(out_done, 16)
            sp.dma_start(out[(NT - 1) * P:N, :], xs[0:LAST, NT - 1, :]).then_inc(out_done, 16)
            sp.wait_ge(out_done, 16 * (NG + 1))

        @block.gpsimd
        def _(pool):
            pool.memset(xs[:, NT - 1, :], 0.0).then_inc(x_pad0, 1)
            pool.memset(keys_s[:], 0.0).then_inc(keys_zero, 1)
            pool.memset(zero_pool[:], 0)
            pool.memset(att_w, 0.0)
            pool.memset(att_b, 0.0).then_inc(attb_zero, 1)
            pool.memset(ident[:], 0.0).then_inc(const_ready, 1)
            pool.memset(ident_b[:], 0.0).then_inc(const_ready, 1)
            pool.wait_ge(const_ready, 2)
            for m in (ident, ident_b):
                pool.affine_select(out=m[:], in_=m[:], compare_op=ALU.not_equal, fill=1.0, base=0,
                                   pattern=[[-1, P]], channel_multiplier=1).then_inc(const_ready, 1)
            kw = dict(allow_small_or_imprecise_dtypes=True)
            pool.iota(iota_row[:], [[1, P]], base=0, channel_multiplier=0, **kw).then_inc(const_ready, 1)
            pool.iota(iota_row_b[:], [[1, P]], base=0, channel_multiplier=0, **kw).then_inc(const_ready, 1)
            pool.iota(iota_part[:], [[0, 1]], base=0, channel_multiplier=1, **kw).then_inc(const_ready, 1)
            pool.iota(win_base[:], [[P, NT + 1]], base=0, channel_multiplier=0, **kw).then_inc(const_ready, 1)
            pool.iota(win_node[:], [[P, NT + 1]], base=0, channel_multiplier=1, **kw).then_inc(const_ready, 1)
            pool.iota(visits_n, [[1, MAXV]], base=0, channel_multiplier=0, **kw).then_inc(const_ready, 1)
            pool.wait_ge(const_ready, 10)
            pool.wait_ge(xl_out, 16)
            pool.sem_inc(idx_seen, 2)
            phase(pool, 1)

            def pool_front(at):
                v, n, par = at.v, at.n, at.par
                for b in range(2):
                    if b == 0:
                        pool.wait_ge(idx_in[par], 16 * n + 16)
                    pool.wait_ge(g_free[b], v + 1)
                    pace = pool.tensor_tensor(pace_pool[:, 2 * par + b:2 * par + b + 1], zero_pool[:], zero_pool[:], ALU.add)
                    if b == 1:
                        pace.then_inc(idx_seen, 1)
                    for t in range(b * HT, b * HT + HT):
                        pool.indirect_dma_start(gath[par][:, t, :], None, xl_dram[:, :],
                                                bass.IndirectOffsetOnAxis(ap=idx[par][:, t:t + 1], axis=0)).then_inc(g_in[par][b], 16)

            run_visits(pool, lambda at, after: pool_front(at), lambda at, before, after: pool_front(at), lambda at: None)
            phase(pool, 2)
            phase(pool, 3)

            def load_down(q):
                pool.dma_start(dn_s[q], down_t[:, q * EB * P:(q + 1) * EB * P].rearrange("(k p) n -> p k n", p=P))\
                    .then_inc(dn_in[q], 16)

            def load_up(q):
                pool.dma_start(up_s[q], up[q * EB * P:(q + 1) * EB * P, :].rearrange("(k p) n -> p k n", p=P))\
                    .then_inc(up_in[q], 16)

            load_down(0)
            pool.wait_ge(q_ps, NG)
            load_up(0)
            pool.wait_ge(g_ps, NG)
            load_down(1)
            pool.wait_ge(u_ps, NG)
            load_up(1)
            pool.wait_ge(mlp_ps, NG)
            load_down(2)
            phase(pool, 4)
            pool.wait_ge(d_ps, NG)
            load_up(2)
            pool.wait_ge(yx_ps, NG)
            load_down(3)
            pool.wait_ge(d_ps, 2 * NG)
            load_up(3)

        @block.scalar
        def _(act):
            act.sem_inc(xnt_ready, 1)
            for n, t in enumerate((slice(0, 2), slice(2, NT))):
                act.wait_ge(var_ready, 2 * n + 1)
                act.activation(nrm[:, 1, t], nrm[:, 0, t], ACT.Sqrt).then_inc(sd_ready, 1)
                act.wait_ge(var_ready, 2 * n + 2)
                act.activation(nrm[:, 3, t], nrm[:, 2, t], ACT.Sqrt).then_inc(sd_ready, 1)
                if n == 0:
                    act.wait_ge(xnt_ps, 1)
                    act.activation(xnt.rearrange("p k c -> p (k c)"), banks(0, 4), ACT.Copy).then_inc(xnt_ready, 1)
            with act.Fori(1, NG) as g:
                act.wait_ge(xnt_ps, g + 1)
                act.activation(xnt.rearrange("p k c -> p (k c)"), banks(0, 4), ACT.Copy).then_inc(xnt_ready, 1)
            act.wait_ge(sz_ready, 1)
            act.activation(p_self, p_self, ACT.Exp).then_inc(sp_ready, 1)
            act.wait_ge(tab_ready, 3)
            phase(act, 1)

            def act_scaled(v, b):
                act.wait_ge(msg_ps[b], v + 1)
                act.activation(lrelu_t[:, b, :], banks(2 * b, 2), ACT.Copy, scale=0.2).then_inc(scaled_ready[b], 1)

            def act_scores(v):
                act.wait_ge(e_ps, v + 1)
                act.activation(e_row_b[0:EH, :], ps[0:EH, 4, 0:P], ACT.Copy)
                act.activation(e_row[0:EH, :], ps[0:EH, 4, 0:P], ACT.Copy).then_inc(e_copied, 1)
                act.wait_ge(fold_done, v + 1)
                for k in range(2 * HEADS):
                    act.wait_ge(bc_ps, 8 * v + k + 1)
                    act.activation(score_r[:, k // HEADS, (k % HEADS) * HT * P:(k % HEADS + 1) * HT * P], banks(ROW_BANK[k % 3]), ACT.Copy)\
                        .then_inc(bc_copied, 1)

            def act_factor(v):
                act.wait_ge(m_ready, v + 1)
                act.activation(m_s, m_d, ACT.Exp).then_inc(ms_ready, 1)

            def act_weights(v):
                act.wait_ge(z_ready, v + 1)
                act.activation(wgt.rearrange("p t (h s) -> p (t h) s", s=SLOT)[:, :, HD], z_e, ACT.Exp).then_inc(p_ready, 1)

            def act_front(at, after):
                act_scaled(at.v, 0)
                act_scaled(at.v, 1)
                act_scores(at.v)

            def act_both(at, before, after):
                act_scaled(at.v, 0)
                act_factor(before.v)
                act_scaled(at.v, 1)
                act_weights(before.v)
                act_scores(at.v)

            def act_last(at):
                act_factor(at.v)
                act_weights(at.v)

            run_visits(act, act_front, act_both, act_last)
            phase(act, 2)

            def act_turned_outputs(g):
                act.wait_ge(ot_ps, g + 1)
                act.activation(o_t.rearrange("p k c -> p (k c)"), banks(0), ACT.Copy).then_inc(ot_ready, 1)

            def act_norm(g):
                act.wait_ge(var2_ready, g + 1)
                act.activation(var_g, var_g, ACT.Sqrt).then_inc(sd2_ready, 1)
                act.wait_ge(ht_ps, g + 1)
                act.activation(pace_act[:], iota_part[:], ACT.Copy)
                act.activation(ht[:, :, bass.ds(g * GT, GT)], banks(4, 4).rearrange("p (k c) -> p k c", k=KD), ACT.Copy)
                act.drain()
                act.sem_inc(ht_ready, 1)

            act_turned_outputs(0)
            act_turned_outputs(1)
            with act.Fori(0, NG - 2) as g:
                act_norm(g)
                act_turned_outputs(g + 2)
            act_norm(NG - 2)
            act_norm(NG - 1)
            phase(act, 3)
            act.sem_inc(qt_ready, 1)
            act.sem_inc(sim_ready, 2)

            def act_queries(n):
                act.wait_ge(q_ps, n)
                act.activation(qt.rearrange("p j c -> p (j c)"), banks(0, 2), ACT.Copy).then_inc(qt_ready, 1)

            def act_exponents(g, i):
                ey, rr, thr, ex, cl = parts(comp)
                act.wait_ge(ex_in_ready, 2 * g + i + 1)
                act.activation(ey, ey, ACT.Exp)
                act.activation(ex, ex, ACT.Exp)
                act.activation(e8.rearrange("p a n -> p (a n)"), e8.rearrange("p a n -> p (a n)"), ACT.Exp)\
                    .then_inc(ex_ready, 1)

            def act_group(g, last=False):
                for i in range(2):
                    act.wait_ge(sim_ps, 2 * g + i + 1)
                    act.wait_ge(sim_free, 2 * g + i + 1)
                    act.activation(sim[:, i, :, :].rearrange("p a n -> p (a n)"), banks(6 * (1 - i), 2), ACT.Copy)\
                        .then_inc(sim_ready, 1)
                act.wait_ge(g_ps, g + 1)
                act.activation(sg, banks(2, 2), ACT.Silu).then_inc(silu_ready, 1)
                act_exponents(g, 0)
                if not last:
                    act_queries(g + 2)
                act_exponents(g, 1)

            act_queries(1)
            with act.Fori(0, NG - 1) as g:
                act_group(g)
            act_group(NG - 1, last=True)
            phase(act, 4)
            act.sem_inc(st_ready, 1)
            act.sem_inc(sd_act, 1)
            for q in range(QE):
                with act.Fori(0, NG) as g:
                    act.wait_ge(v_ready, NG * q + g + 1)
                    act.wait_ge(d_ps, NG * q + g + 1)
                    act.activation(sd_t.rearrange("p b c -> p (b c)"), banks(6, 2), ACT.Silu).then_inc(sd_act, 1)
                    act.wait_ge(st_ps, NG * q + g + 1)
                    act.activation(s_t.rearrange("p b c -> p (b c)"), banks(0, 2), ACT.Copy).then_inc(st_ready, 1)

        @block.vector
        def _(dve):
            dve.wait_ge(const_ready, 10)
            dve.memset(one_c, 1.0)
            dve.tensor_scalar(ext_c[:, 2:3], iota_part[:], 1.0, None, ALU.add)
            dve.tensor_scalar(ext_c[:, 3:4], iota_part[:], -1.0, float(NCH), ALU.mult, ALU.add)
            dve.wait_ge(dst_in, 16)
            dve.tensor_copy(dcol, dst_i)
            dve.drain()
            dcol_v = dcol.rearrange("p (c t) -> p c t", t=T)
            dve.tensor_reduce(ext_p[:, 0:NCH], dcol_v, AX.X, ALU.max)
            dve.tensor_reduce(ext_p[:, NCH:2 * NCH], dcol_v, AX.X, ALU.min).then_inc(bnd_ready, 1)
            dve.wait_ge(bnd_ps, 1)
            dve.tensor_reduce(ext_c[0:NCH, 0:1], ps[0:NCH, 7, 0:P], AX.X, ALU.max)
            dve.tensor_reduce(ext_c[0:NCH, 1:2], ps[0:NCH, 7, P:2 * P], AX.X, ALU.min)
            dve.drain()
            may = bnd_p[0:NCH, 0:NT]
            dve.tensor_scalar(may, win_base[0:NCH, 0:NT], ext_c[0:NCH, 0:1], None, ALU.is_le)
            dve.drain()
            dve.scalar_tensor_tensor(may, win_base[0:NCH, 1:NT + 1], ext_c[0:NCH, 1:2], may, ALU.is_gt, ALU.mult)
            dve.drain()
            dve.tensor_scalar(bnd_p[0:NCH, NT:2 * NT], may, ext_c[0:NCH, 3:4], None, ALU.mult)
            dve.drain()
            dve.tensor_scalar(may, may, ext_c[0:NCH, 2:3], None, ALU.mult).then_inc(bnd_ready, 1)
            dve.wait_ge(bnd_ps, 2)
            dve.tensor_reduce(bnd_t[0:2 * NT, 0:1], ps[0:2 * NT, 7, 0:NCH], AX.X, ALU.max).then_inc(bnd_ready, 1)
            dve.wait_ge(bnd_ps, 3)
            r0 = bnd_r[0:1, :, :]
            dve.tensor_scalar(r0[:, 1, :], ps[0:1, 7, P:P + NT], 1.0, None, ALU.max)
            dve.tensor_scalar(r0[:, 0, :], ps[0:1, 7, P + NT:P + 2 * NT], -1.0, float(NCH), ALU.mult, ALU.add)
            dve.drain()
            dve.tensor_scalar(r0[:, 2, :], r0[:, 1, :], -1.0, None, ALU.add)
            dve.drain()
            dve.tensor_tensor(r0[:, 0, :], r0[:, 0, :], r0[:, 2, :], ALU.min)
            dve.drain()
            dve.tensor_tensor(r0[:, 2, :], r0[:, 1, :], r0[:, 0, :], ALU.subtract)
            dve.memset(r0[:, 3, 0:1], 1.0)
            dve.drain()
            for w in range(NT - 1):
                dve.tensor_tensor(r0[:, 3, w + 1:w + 2], r0[:, 3, w:w + 1], r0[:, 2, w:w + 1], ALU.add)
                dve.drain()
            dve.tensor_tensor(r0[:, 1, :], r0[:, 0, :], r0[:, 3, :], ALU.subtract)
            dve.tensor_tensor(r0[:, 4, 0:1], r0[:, 3, NT - 1:NT], r0[:, 2, NT - 1:NT], ALU.add)
            dve.drain()
            vf = visits_f[0:1, :, :]
            dve.tensor_copy(r0[:, 2, 0:1], r0[:, 1, 0:1])
            dve.tensor_tensor(r0[:, 2, 1:NT], r0[:, 1, 1:NT], r0[:, 1, 0:NT - 1], ALU.subtract)
            dve.drain()
            dve.sem_inc(tab_ready, 1)
            dve.wait_ge(tab_ps, 1)
            dve.tensor_copy(first_c[0:NT, :], ps[0:NT, 7, 0:2])
            dve.drain()
            begun = visits_f[0:NT, 2, :]
            dve.tensor_scalar(begun, visits_n[0:NT, :], 1.0, first_c[0:NT, 0:1], ALU.add, ALU.is_ge)
            dve.drain()
            dve.sem_inc(tab_ready, 1)
            dve.wait_ge(tab_ps, 2)
            dve.tensor_scalar(vf[:, 0, :], ps[0:1, 6, 0:MAXV], float(-NT - 1), None, ALU.add)
            dve.scalar_tensor_tensor(vf[:, 1, :], visits_n[0:1, :], 1.0, ps[0:1, 5, 0:MAXV], ALU.add, ALU.add)
            dve.drain()
            dve.tensor_scalar(vf[:, 2, :], visits_n[0:1, :], 1.0, r0[:, 4, 0:1], ALU.add, ALU.is_lt)
            dve.drain()
            dve.tensor_tensor(vf[:, 1, :], vf[:, 1, :], vf[:, 2, :], ALU.mult)
            dve.tensor_tensor(vf[:, 0, :], vf[:, 0, :], vf[:, 2, :], ALU.mult)
            dve.tensor_scalar(r0[:, 4, 1:2], r0[:, 4, 0:1], 0.5, None, ALU.mult)
            dve.drain()
            dve.tensor_scalar(vf[:, 0, :], vf[:, 0, :], float(NT), None, ALU.add)
            dve.tensor_scalar(vf[:, 2, :], visits_n[0:1, :], 1.0, r0[:, 4, 1:2], ALU.add, ALU.is_le)
            dve.drain()
            dve.tensor_reduce(r0[:, 4, 2:3], vf[:, 2, :], AX.X, ALU.add)
            dve.tensor_copy(visits[0:1, :, :], vf[:, 0:2, :])
            dve.drain()
            dve.tensor_scalar(n_pairs[0:1, 1:2], r0[:, 4, 2:3], -1.0, None, ALU.add)
            dve.drain()
            dve.tensor_copy(n_pairs[0:1, 0:1], r0[:, 4, 2:3]).then_inc(tab_ready, 1)

            def dve_statistics(groups):
                t0, t1 = 2 * groups[0], 2 * groups[-1] + 2
                for g in groups:
                    dve.wait_ge(x_in[g], 16)
                    if g == NG - 1:
                        dve.wait_ge(x_tail, 16)
                    for t in (2 * g, 2 * g + 1):
                        for a in range(2):
                            dve.bn_stats(stats[:, t, a, :], xs[:, t, a * 512:a * 512 + 512])
                dve.drain()
                for t in range(t0, t1):
                    dve.bn_aggr(meanvar[:, t, :], stats[:, t, :, :].rearrange("p a s -> p (a s)"))
                dve.drain()
                n = nrm[:, :, t0:t1]
                dve.tensor_scalar(n[:, 0, :], meanvar[:, t0:t1, 1], 1e-5, None, ALU.add).then_inc(var_ready, 1)
                dve.wait_ge(sd_ready, 1 if t0 == 0 else 3)
                dve.reciprocal(n[:, 1, :], n[:, 1, :])
                dve.drain()
                dve.tensor_tensor(n[:, 2, :], n[:, 1, :], n[:, 1, :], ALU.mult)
                dve.drain()
                dve.tensor_tensor(n[:, 2, :], n[:, 2, :], meanvar[:, t0:t1, 1], ALU.mult)
                dve.drain()
                dve.tensor_scalar(n[:, 2, :], n[:, 2, :], 1e-6, None, ALU.add).then_inc(var_ready, 1)
                dve.wait_ge(sd_ready, 2 if t0 == 0 else 4)
                dve.reciprocal(n[:, 3, :], n[:, 3, :])
                dve.drain()
                dve.tensor_tensor(n[:, 3, :], n[:, 3, :], n[:, 1, :], ALU.mult)
                dve.drain()

            def dve_normalised(g):
                if not isinstance(g, int):
                    dve.wait_ge(xnt_ps, g)
                for i in range(2):
                    t = bass.ds(2 * g + i, 1)
                    last = dve.tensor_scalar(xn[:, i, :], xs[:, t, :].rearrange("p o d -> p (o d)"),
                                             meanvar[:, t, 0], nrm[:, 3, t], ALU.subtract, ALU.mult)
                last.then_inc(xn_ready, 1)

            def dve_z(g):
                dve.wait_ge(zt_ps, g + 1)
                dve.tensor_copy(zt.rearrange("p k c -> p (k c)"), banks(4)).then_inc(zt_ready, 1)

            def dve_projected(g):
                dve.wait_ge(xlr_ps, g + 1)
                dve.tensor_scalar(xl[:, bass.ds(2 * g, 2), :], ps[:, 5:7, 0:HID], 1.0, None, ALU.mult)
                dve.tensor_scalar(xr[:, bass.ds(2 * g, 2), :], ps[:, 5:7, HID:2 * HID], 1.0, None, ALU.mult)
                dve.drain()

            def dve_self_scores(g):
                t2 = bass.ds(2 * g, 2)
                dve.tensor_tensor(self_m, xl[:, t2, :], xr[:, t2, :], ALU.add)
                dve.drain()
                dve.scalar_tensor_tensor(self_m, self_m, 0.2, self_m, ALU.mult, ALU.max)
                dve.drain()
                dve.tensor_tensor(self_m, self_m, att_s.rearrange("p (o n) -> p o n", o=1).broadcast_to((P, 2, HID)), ALU.mult)
                dve.drain()
                dve.tensor_reduce(e_self[:, bass.ds(2 * g * HEADS, 2 * HEADS)], self_m.rearrange("p t (h d) -> p (t h) d", h=HEADS), AX.X, ALU.add)

            def dve_split_xr(g):
                t2 = bass.ds(2 * g, 2)
                dve.tensor_scalar(xr3[:, t2, 0, :], xr[:, t2, :], 1.0, None, ALU.mult)
                dve.drain()
                dve.tensor_tensor(xr_rest, xr[:, t2, :], xr3[:, t2, 0, :], ALU.subtract)
                dve.drain()
                dve.tensor_scalar(xr3[:, t2, 1, :], xr_rest, 1.0, None, ALU.mult)
                dve.drain()
                dve.tensor_tensor(xr3[:, t2, 2, :], xr_rest, xr3[:, t2, 1, :], ALU.subtract)
                dve.drain()

            dve_statistics([0])
            dve_normalised(0)
            dve.wait_ge(gw_in, 64)
            for k in range(KD):
                last = dve.tensor_scalar(wdn_s[:, k, :], wdn_s[:, k, :], rms_s[:, k:k + 1], None, ALU.mult)
            last.then_inc(wdn_scaled, 1)
            dve_statistics(list(range(1, NG)))
            dve.wait_ge(ew_in, 16)
            dve.wait_ge(xnt_ps, 1)
            dve_normalised(1)
            with dve.Fori(0, NG - 2) as g:
                dve_z(g)
                dve_normalised(g + 2)
                dve_projected(g)
                dve_self_scores(g)
                dve_split_xr(g)
            for g in (NG - 2, NG - 1):
                dve_z(g)
                dve_projected(g)
                if g == NG - 1:
                    dve.sem_inc(xl_ready, 1)
                dve_self_scores(g)
                dve_split_xr(g)
            dve.drain()
            dve.wait_ge(attb_zero, 1)
            dve.wait_ge(attb_in, 16 * HEADS)
            for t in range(T):
                last = dve.tensor_copy(att_w[:, :, t, t * HEADS:(t + 1) * HEADS], att_b)
            last.then_inc(attw_ready, 1)
            dve.tensor_copy(m_self, e_self)
            dve.memset(m_all[:, NT, :], 0.0)
            dve.memset(acc_all[:, NT, :, :], 0.0)
            dve.memset(xr3[:, NT, :, :], 0.0)
            dve.drain()
            dve.tensor_copy(m_all[:, 0:NT, :].rearrange("p t h -> p (t h)"), m_self)
            dve.tensor_tensor(p_self, e_self, m_self, ALU.subtract).then_inc(sz_ready, 1)
            dve.wait_ge(sp_ready, 1)
            p_b = p_self.rearrange("p (t h o) -> p t h o", h=HEADS, o=1)
            for t in range(NT):
                dve.tensor_tensor(acc_all[:, t, :, 0:HD], xl[:, t, :].rearrange("p (h d) -> p h d", h=HEADS),
                                  p_b[:, t, :, :].broadcast_to((P, HEADS, HD)), ALU.mult)
            dve.tensor_copy(acc_all[:, 0:NT, :, :].rearrange("p t h s -> p (t h) s")[:, :, HD], p_self)
            for s in (drow_free, idx_free, idx_free, *g_free, *g_free, fold_done):
                dve.sem_inc(s, 1)
            phase(dve, 1)

            def dve_one_hots(at):
                at.load_window(dve)
                at.load_chunk(dve)
                v, w, c, par = at.v, at.w, at.c, at.par
                dve.wait_ge(drow_in, 16 * v + 16)
                dve.tensor_scalar(oh_d[par], drow, win_node[:, bass.ds(w, 1)], None, ALU.is_equal)
                dve.tensor_scalar(xr_w[par].rearrange("p s n -> p (s n)"), xr3[:, bass.ds(w, 1), :, :].rearrange("p o s n -> p (o s n)"),
                                  1.0, None, ALU.mult).then_inc(ohd_ready, 1)
                dve.tensor_scalar(dcol_c[par], dcol[:, bass.ds(c * T, T)], win_base[:, bass.ds(w, 1)], None, ALU.subtract)
                dve.drain()
                dve.sem_inc(drow_free, 1)

            def dve_maxima(at):
                v, w = at.v, at.w
                m_wv = m_all[:, bass.ds(w, 1), :].rearrange("p o h -> p (o h)")
                n = HT * P
                dve.drain()
                dve.wait_ge(bc_copied, 8 * v + 8)
                dve.tensor_tensor(fold.rearrange("p h n -> p (h n)"), score_r[:, 0, :], score_r[:, 1, :], ALU.max)
                dve.drain()
                dve.sem_inc(fold_done, 1)
                for q in (2, 4):
                    dve.tensor_tensor(fold[:, :, 0:n // q], fold[:, :, 0:n // q], fold[:, :, n // q:2 * n // q], ALU.max)
                    dve.drain()
                dve.tensor_reduce(cmax, fold[:, :, 0:n // 4], AX.X, ALU.max)
                dve.drain()
                dve.tensor_tensor(m_n, cmax, m_wv, ALU.max)
                dve.drain()
                dve.tensor_scalar(m_neg, m_n, -1.0, None, ALU.mult).then_inc(mw_ready, 1)
                dve.tensor_tensor(m_d, m_wv, m_n, ALU.subtract).then_inc(m_ready, 1)
                dve.drain()
                dve.tensor_copy(m_wv, m_n)

            def dve_exponents(v):
                dve.wait_ge(z_ps, v + 1)
                dve.tensor_scalar(z_e, ps[:, 7, SUMS:SUMS + T * HEADS], 80.0, None, ALU.min).then_inc(z_ready, 1)

            def dve_weigh(par, v, b):
                h = slice(b * HT, (b + 1) * HT)
                wv = wgt[:, h, :].rearrange("p t (h s) -> p (t h) s", s=SLOT)
                if b == 0:
                    dve.wait_ge(p_ready, v + 1)
                dve.tensor_tensor(wv[:, :, 0:HD], gath[par][:, h, :].rearrange("p t (h d) -> p (t h) d", h=HEADS),
                                  wv[:, :, HD:SLOT].broadcast_to((P, HT * HEADS, HD)), ALU.mult).then_inc(wg_ready[b], 1)
                dve.drain()
                dve.sem_inc(g_free[b], 1)

            def dve_lrelu(v, b):
                dve.wait_ge(scaled_ready[b], v + 1)
                dve.tensor_tensor(lrelu_t[:, b, :], lrelu_t[:, b, :], banks(2 * b, 2), ALU.max).then_inc(lrelu_ready[b], 1)
                if b == 1:
                    dve.sem_inc(idx_free, 1)

            def dve_mask(par, v):
                dve.tensor_scalar(mask, oh_d[par], -1.0, BIG, ALU.add, ALU.mult).then_inc(mask_ready, 1)

            def dve_mask_rows(v):
                dve.wait_ge(bc_copied, 8 * v + HEADS)
                rows = score_r[:, 0, :].rearrange("p (h n) -> p h n", h=HEADS)
                dve.tensor_tensor(rows, rows, mask[:, 0:HT * P].rearrange("p (h n) -> p h n", h=1)
                                  .broadcast_to((P, HEADS, HT * P)), ALU.add)

            def dve_sums(at):
                v, w = at.v, at.w
                av = acc_all[:, bass.ds(w, 1), :, :].rearrange("p o h s -> p (o h) s")
                dve.wait_ge(ms_ready, v + 1)
                dve.tensor_tensor(av, av, m_s.rearrange("p (h o) -> p h o", o=1).broadcast_to((P, HEADS, SLOT)), ALU.mult)
                dve.drain()
                dve.wait_ge(sc_ps, v + 1)
                dve.tensor_tensor(av, av, ps[:, 7, 0:HEADS * SLOT].rearrange("p (h s) -> p h s", h=HEADS), ALU.add)
                dve.drain()

            def dve_edge_hots(par):
                for t in range(T):
                    last = dve.tensor_scalar(oh_e[par][:, t, :], iota_row[:], dcol_c[par][:, t:t + 1], None, ALU.is_equal)

            def dve_front(at, after):
                dve_one_hots(at)
                dve_lrelu(at.v, 0)
                dve_lrelu(at.v, 1)
                dve_mask(at.par, at.v)
                dve_edge_hots(at.par)
                dve_one_hots(after)

            def dve_both(at, before, after):
                if before.w is None:
                    before.load_window(dve)
                dve_mask_rows(before.v)
                dve_maxima(before)
                dve_lrelu(at.v, 0)
                dve_exponents(before.v)
                dve_lrelu(at.v, 1)
                dve_weigh(before.par, before.v, 0)
                dve_weigh(before.par, before.v, 1)
                dve_mask(at.par, at.v)
                dve_edge_hots(at.par)
                if after is not None:
                    dve_one_hots(after)
                if at.w is None:
                    at.load_window(dve)
                dve_sums(before)

            def dve_last(at):
                dve_mask_rows(at.v)
                dve_maxima(at)
                dve_exponents(at.v)
                dve_weigh(1, at.v, 0)
                dve_weigh(1, at.v, 1)
                dve_sums(at)

            run_visits(dve, dve_front, dve_both, dve_last)
            phase(dve, 2)

            def dve_outputs(g):
                t2 = bass.ds(2 * g, 2)
                dve.tensor_scalar(rden, acc_all[:, t2, :, HD], 1e-16, None, ALU.add)
                dve.drain()
                dve.reciprocal(rden, rden)
                dve.drain()
                for i in range(2):
                    last = dve.tensor_tensor(o_s[:, i, :].rearrange("p (h d) -> p h d", h=HEADS),
                                             acc_all[:, bass.ds(2 * g + i, 1), :, 0:HD].rearrange("p o h d -> p (o h) d"),
                                             rden[:, i, :].rearrange("p (h o) -> p h o", o=1).broadcast_to((P, HEADS, HD)), ALU.mult)
                last.then_inc(o_ready, 1)

            def dve_residual_and_norm(g, last_group=False):
                t2 = bass.ds(2 * g, 2)
                if not last_group:
                    dve.wait_ge(ot_ps, g + 1)
                    dve_outputs(g + 1)
                dve.wait_ge(y_ps, g + 1)
                dve.tensor_tensor(xs[:, t2, :].rearrange("p t d -> p (t d)"), xs[:, t2, :].rearrange("p t d -> p (t d)"),
                                  banks(0, 4), ALU.add).then_inc(x1_ready, 1)
                dve.drain()
                for i in range(2):
                    for a in range(2):
                        dve.bn_stats(stats_g[:, i, a, :], xs[:, bass.ds(2 * g + i, 1), a * 512:a * 512 + 512].rearrange("p o d -> p (o d)"))
                dve.drain()
                for i in range(2):
                    dve.bn_aggr(meanvar_g[:, i, :], stats_g[:, i, :, :].rearrange("p a s -> p (a s)"))
                dve.drain()
                dve.tensor_scalar(var_g, meanvar_g[:, :, 1], 1e-5, None, ALU.add).then_inc(var2_ready, 1)
                dve.wait_ge(sd2_ready, g + 1)
                dve.reciprocal(rstd_g, var_g)
                dve.drain()
                for i in range(2):
                    if i == 0:
                        dve.wait_ge(ht_ready, g + 1)
                    last = dve.tensor_scalar(h_s[:, i, :], xs[:, bass.ds(2 * g + i, 1), :].rearrange("p o d -> p (o d)"),
                                             meanvar_g[:, i, 0:1], rstd_g[:, i:i + 1], ALU.subtract, ALU.mult)
                last.then_inc(h_ready, 1)

            dve_outputs(0)
            with dve.Fori(0, NG - 1) as g:
                dve_residual_and_norm(g)
            dve_residual_and_norm(NG - 1, last_group=True)
            phase(dve, 3)

            def pairs_of(m):
                return (m[:, 0:HEADS, :].rearrange("p h (a o) -> p h a o", o=1).broadcast_to((P, HEADS, TOP, TOP)),
                        m[:, HEADS:KEYP, :].rearrange("p h (o b) -> p h o b", o=1).broadcast_to((P, HEADS, TOP, TOP)))

            dve.sem_inc(sim_free, 2)
            dve.sem_inc(mlp_added, 1)
            dve.sem_inc(comp_out, 16)
            with dve.Fori(0, NG) as g:
                for i in range(2):
                    if i == 1:
                        dve.wait_ge(silu_ready, g + 1)
                        dve.wait_ge(u_ps, g + 1)
                        dve.tensor_tensor(a_t.rearrange("p k c -> p (k c)"), sg, banks(4, 2), ALU.mult).then_inc(at_ready, 1)
                    sx, sy = sim[:, i, 0:HEADS, :], sim[:, i, HEADS:KEYP, :]
                    ey, rr, thr, ex, cl = parts(comp)
                    dve.drain()
                    dve.wait_ge(sim_ready, 2 * g + i + 3)
                    dve.memset(pace_dve[:], 0.0)
                    dve.drain()
                    for a in range(KEYP):
                        dve.max(s8[:, a, :], sim[:, i, a, :])
                    dve.drain()
                    for a in range(KEYP):
                        dve.max_index(i8[:, a, :], s8[:, a, :], sim[:, i, a, :])
                    dve.tensor_tensor(grid.rearrange("p (h a b) -> p h a b", h=HEADS, a=TOP), *pairs_of(s8), ALU.add)
                    dve.tensor_tensor(e8, s8, s8[:, :, 0:1].broadcast_to((P, KEYP, TOP)), ALU.subtract)
                    dve.wait_ge(comp_out, 32 * g + 16 * i + 16)
                    dve.tensor_tensor(ey, sy, s8[:, HEADS:KEYP, 0:1].broadcast_to((P, HEADS, NK)), ALU.subtract)
                    dve.tensor_tensor(ex, sx[:, :, 0:NX], s8[:, 0:HEADS, 0:1].broadcast_to((P, HEADS, NX)), ALU.subtract)\
                        .then_inc(ex_in_ready, 1)
                    dve.drain()
                    dve.sem_inc(sim_free, 1)
                    dve.tensor_copy(i8f, i8)
                    for h in range(HEADS):
                        dve.max(g8[:, h, :], grid[:, h * 64:h * 64 + 64])
                    dve.drain()
                    for h in range(HEADS):
                        dve.match_replace(grid_r[:, h * 64:h * 64 + 64], g8[:, h, :], grid[:, h * 64:h * 64 + 64], -BIG)
                    dve.drain()
                    dve.tensor_tensor(sel, grid_r, grid, ALU.not_equal)
                    dve.drain()
                    dve.tensor_reduce(n_i, sel.rearrange("p (a b) -> p a b", b=TOP), AX.X, ALU.add)
                    for j in range(TOP):
                        for h in range(HEADS):
                            dve.tensor_scalar(ranks[:, j, h, :], iota_row_b[:], i8f[:, HEADS + h, j:j + 1], float(TOP - j),
                                              ALU.is_equal, ALU.mult)
                    dve.tensor_tensor(at_first, iota_row[:, 0:NX].rearrange("p (h x a) -> p h x a", h=1, a=1).broadcast_to((P, HEADS, NX, TOP)),
                                      i8f[:, 0:HEADS, :].rearrange("p h (x a) -> p h x a", x=1).broadcast_to((P, HEADS, NX, TOP)), ALU.is_equal)
                    dve.drain()
                    dve.tensor_tensor(ranks[:, 0:4, :, :], ranks[:, 0:4, :, :], ranks[:, 4:8, :, :], ALU.add)
                    dve.tensor_tensor(at_first, at_first, n_i.rearrange("p (h x a) -> p h x a", h=HEADS, x=1)
                                      .broadcast_to((P, HEADS, NX, TOP)), ALU.mult)
                    dve.drain()
                    dve.tensor_tensor(ranks[:, 0:2, :, :], ranks[:, 0:2, :, :], ranks[:, 2:4, :, :], ALU.add)
                    dve.tensor_reduce(thr, at_first, AX.X, ALU.add)
                    dve.drain()
                    dve.tensor_tensor(rr, ranks[:, 0, :, :], ranks[:, 1, :, :], ALU.add)
                    dve.tensor_scalar(thr, thr, -1.0, float(TOP + 1), ALU.mult, ALU.add)
                    dve.wait_ge(ex_ready, 2 * g + i + 1)
                    dve.tensor_tensor(wsel.rearrange("p (h a b) -> p h a b", h=HEADS, a=TOP), *pairs_of(e8), ALU.mult)
                    dve.drain()
                    dve.tensor_tensor(wsel, wsel, sel, ALU.mult)
                    dve.drain()
                    dve.tensor_reduce(r_i, wsel.rearrange("p (a b) -> p a b", b=TOP), AX.X, ALU.add)
                    dve.drain()
                    dve.tensor_reduce(z_h, r_i.rearrange("p (h a) -> p h a", a=TOP), AX.X, ALU.add)
                    dve.drain()
                    dve.reciprocal(rz, z_h)
                    dve.drain()
                    rzb = rz.rearrange("p (h o) -> p h o", o=1)
                    dve.tensor_tensor(ex, ex, rzb.broadcast_to((P, HEADS, NX)), ALU.mult)
                    rv = r_i.rearrange("p (h a) -> p h a", a=TOP)
                    dve.tensor_tensor(rv, rv, rzb.broadcast_to((P, HEADS, TOP)), ALU.mult)
                    nv = n_i.rearrange("p (h a) -> p h a", a=TOP)
                    dve.tensor_scalar(nv, i8f[:, 0:HEADS, :], float(NX), None, ALU.is_ge)
                    dve.drain()
                    dve.tensor_tensor(nv, nv, rv, ALU.mult)
                    dve.drain()
                    dve.tensor_reduce(cl, n_i, AX.X, ALU.add)
                    dve.drain()
                    dve.sem_inc(comp_ready, 1)
                dve.wait_ge(mlp_ps, g + 1)
                xv = xs[:, bass.ds(2 * g, 2), :].rearrange("p t d -> p (t d)")
                dve.tensor_tensor(xv, xv, banks(2, 4), ALU.add).then_inc(mlp_added, 1)
            phase(dve, 4)

            dve.sem_inc(cmp_free, 2)
            dve.sem_inc(yx_added, 1)
            dve.sem_inc(v_ready, 1)

            def dve_expert_weights(m, q):
                for i in range(2):
                    ey, rr, thr, ex, cl = parts(cmp_in[:, i, :])
                    for b in range(EB):
                        for h in range(HEADS):
                            if b == 0 and h == 0:
                                dve.wait_ge(cmp_in_s[i], 16 * m + 16)
                                dve.wait_ge(st_ready, m + 1)
                            k = EB * q + b
                            dve.scalar_tensor_tensor(s_tmp[:, b, h, :], rr[:, h, :], thr[:, h, k:k + 1], ey[:, h, :], ALU.is_ge, ALU.mult)
                    dve.drain()
                    for h in range(HEADS):
                        for b in range(EB):
                            k = EB * q + b
                            if h == 0:
                                dve.tensor_scalar(s_q[:, i, b, :], s_tmp[:, b, h, :], ex[:, h, k:k + 1], None, ALU.mult)
                            else:
                                dve.scalar_tensor_tensor(s_q[:, i, b, :], s_tmp[:, b, h, :], ex[:, h, k:k + 1], s_q[:, i, b, :],
                                                         ALU.mult, ALU.add)
                        dve.drain()
                    if q == QE - 1:
                        dve.tensor_tensor(s_q[:, i, EB - 1, NK - 1:NK], s_q[:, i, EB - 1, NK - 1:NK], cl, ALU.add)
                        dve.drain()
                    dve.sem_inc(cmp_free, 1)
                dve.sem_inc(s_ready, 1)

            def dve_weigh_experts(m_1):
                dve.wait_ge(st_ready, m_1 + 1)
                dve.wait_ge(sd_act, m_1 + 1)
                dve.tensor_tensor(v_t.rearrange("p b c -> p (b c)"), sd_t.rearrange("p b c -> p (b c)"),
                                  s_t.rearrange("p b c -> p (b c)"), ALU.mult).then_inc(v_ready, 1)

            def dve_add_experts(m_1, g):
                dve.wait_ge(yx_ps, m_1)
                xv = xs[:, bass.ds(2 * g, 2), :].rearrange("p t d -> p (t d)")
                dve.tensor_tensor(xv, xv, banks(2, 4), ALU.add).then_inc(yx_added, 1)
                dve.drain()

            def dve_experts(m, q, g, before):
                dve_weigh_experts(m)
                dve_expert_weights(m, q)
                dve_add_experts(m, before)

            def dve_experts_last(before):
                dve_weigh_experts(NG * QE)
                dve_add_experts(NG * QE, before)

            run_experts(dve, lambda m, q, g: dve_expert_weights(m, q), dve_experts, dve_experts_last)

        @block.tensor
        def _(pe):
            pe.wait_ge(const_ready, 10)
            pe.wait_ge(bnd_ready, 1)
            pe.transpose(ps[0:NCH, 7, 0:P], ext_p[:, 0:NCH], ident[:])
            pe.transpose(ps[0:NCH, 7, P:2 * P], ext_p[:, NCH:2 * NCH], ident[:]).then_inc(bnd_ps, 1)
            pe.wait_ge(bnd_ready, 2)
            pe.transpose(ps[0:2 * NT, 7, 0:NCH], bnd_p[0:NCH, :], ident[0:NCH, 0:NCH]).then_inc(bnd_ps, 1)
            pe.wait_ge(bnd_ready, 3)
            pe.transpose(ps[0:1, 7, P:P + 2 * NT], bnd_t[0:2 * NT, 0:1], ident[0:2 * NT, 0:2 * NT]).then_inc(bnd_ps, 1)
            pe.wait_ge(tab_ready, 1)
            pe.matmul(ps[0:NT, 7, 0:1], bnd_r[0:1, 3, :], ident[0:1, 0:1], start=True, stop=True)
            pe.matmul(ps[0:NT, 7, 1:2], bnd_r[0:1, 2, :], ident[0:1, 0:1], start=True, stop=True).then_inc(tab_ps, 1)
            pe.wait_ge(tab_ready, 2)
            pe.matmul(ps[0:1, 6, 0:MAXV], one_c[0:NT, :], visits_f[0:NT, 2, :], start=True, stop=True)
            pe.matmul(ps[0:1, 5, 0:MAXV], first_c[0:NT, 1:2], visits_f[0:NT, 2, :], start=True, stop=True).then_inc(tab_ps, 1)

            def pe_turn_x(g):
                pe.wait_ge(xn_ready, g + 1)
                pe.wait_ge(xnt_ready, g + 1)
                for k in range(KD):
                    for i in range(2):
                        a = k * GT + i * P
                        last = pe.transpose(banks(0, 4)[:, a:a + P], xn[:, i, k * P:(k + 1) * P], ident[:])
                last.then_inc(xnt_ps, 1)

            def pe_z(g):
                pe.wait_ge(xnt_ready, g + 2)
                for j in range(KH):
                    for k in range(KD):
                        last = pe.matmul(banks(4)[:, j * GT:(j + 1) * GT], wdn_s[:, k, j * P:(j + 1) * P], xnt[:, k, :],
                                         start=(k == 0), stop=(k == KD - 1))
                last.then_inc(zt_ps, 1)

            def pe_xlr(g):
                pe.wait_ge(zt_ready, g + 1)
                for i in range(2):
                    for k in range(KH):
                        last = pe.matmul(banks(5 + i), zt[:, k, i * P:(i + 1) * P], wlr_s[:, k, :],
                                         start=(k == 0), stop=(k == KH - 1))
                last.then_inc(xlr_ps, 1)

            pe_turn_x(0)
            pe.wait_ge(wdn_scaled, 1)
            with pe.Fori(0, NG - 1) as g:
                pe_z(g)
                pe_turn_x(g + 1)
                pe_xlr(g)
            pe_z(NG - 1)
            pe_xlr(NG - 1)
            pe.wait_ge(tab_ready, 3)
            phase(pe, 1)

            pe.wait_ge(attw_ready, 1)

            def rows_of(m, b):
                return m[:, b * HT * P:(b + 1) * HT * P]

            def pe_destinations(par, at):
                v = at.v
                for b in range(2):
                    if b == 0:
                        pe.wait_ge(ohd_ready, v + 1)
                    if not isinstance(v, int):
                        pe.wait_ge(lrelu_ready[b], v)
                    for k in range(KH):
                        for s in range(3):
                            pe.matmul(banks(2 * b + k),
                                      xr_w[par][:, s, k * P:(k + 1) * P],
                                      rows_of(oh_d[par], b), start=(s == 0), stop=False, skip_group_check=True)

            def pe_sources(par, at, b):
                pe.wait_ge(g_in[par][b], 16 * HT * at.n + 16 * HT)
                for k in range(KH):
                    for t in range(HT):
                        last = pe.matmul(ps[:, 2 * b + k, t * P:(t + 1) * P], gath[par][:, b * HT + t, k * P:(k + 1) * P], ident[:],
                                         start=False, stop=(t == HT - 1), skip_group_check=True)
                last.then_inc(msg_ps[b], 1)

            def pe_scores(v):
                for b in range(2):
                    if b == 0 and not isinstance(v, int):
                        pe.wait_ge(bc_copied, 8 * v)
                    pe.wait_ge(lrelu_ready[b], v + 1)
                    for t in range(HT):
                        for k in range(KH):
                            a = (k * HT + t) * P
                            last = pe.matmul(ps[0:EH, 4, 0:P], att_w[:, k, b * HT + t, :], lrelu_t[:, b, a:a + P],
                                             start=(b == 0 and t == 0 and k == 0), stop=(b == 1 and t == HT - 1 and k == KH - 1))
                last.then_inc(e_ps, 1)

            def pe_score_rows(v, first=0, end=2 * HEADS):
                for k in range(first, end):
                    b, h = k // HEADS, k % HEADS
                    if k == 0:
                        pe.wait_ge(e_copied, v + 1)
                    if k >= 3:
                        pe.wait_ge(bc_copied, 8 * v + k - 2)
                    o = banks(ROW_BANK[k % 3])
                    if b == 1:
                        if k == HEADS:
                            pe.wait_ge(mask_ready, v + 1)
                        pe.matmul(o, ident_b[:], rows_of(mask, b), start=True, stop=False, skip_group_check=True)
                    for t in range(HT):
                        j = (b * HT + t) * HEADS + h
                        last = pe.matmul(o[:, t * P:(t + 1) * P], ident_b[0:EH, j:j + 1].broadcast_to((EH, P)), e_row_b[0:EH, :],
                                         start=(b == 0 and t == 0), stop=(t == HT - 1), skip_group_check=True)
                    last.then_inc(bc_ps, 1)

            def pe_exponents(par, v):
                pe.wait_ge(mw_ready, v + 1)
                pe.matmul(ps[:, 7, SUMS:SUMS + EH], e_row[0:EH, :], ident[0:EH, 0:EH], start=True, stop=False, skip_group_check=True)
                for t in range(T):
                    last = pe.matmul(ps[:, 7, SUMS + t * HEADS:SUMS + (t + 1) * HEADS], oh_d[par][:, t * P:(t + 1) * P], m_neg,
                                     start=False, stop=(t == T - 1), skip_group_check=True)
                last.then_inc(z_ps, 1)

            def pe_sums(par, v, b):
                pe.wait_ge(wg_ready[b], v + 1)
                for t in range(b * HT, (b + 1) * HT):
                    last = pe.matmul(ps[:, 7, 0:SUMS], oh_e[par][:, t, :], wgt[:, t, :], start=(t == 0), stop=(t == T - 1))
                if b == 1:
                    last.then_inc(sc_ps, 1)

            def pe_front(at, after):
                par = at.par
                pe_destinations(par, at)
                pe_sources(par, at, 0)
                pe_sources(par, at, 1)
                pe_scores(at.v)
                pe_score_rows(at.v)

            def pe_both(at, before, after):
                par = at.par
                pe_destinations(par, at)
                pe_sources(par, at, 0)
                pe_sources(par, at, 1)
                pe_exponents(1 - par, before.v)
                pe_scores(at.v)
                pe_sums(1 - par, before.v, 0)
                pe_score_rows(at.v, 0, 3)
                pe_sums(1 - par, before.v, 1)
                pe_score_rows(at.v, 3, 2 * HEADS)

            def pe_last(at):
                pe_exponents(1, at.v)
                pe_sums(1, at.v, 0)
                pe_sums(1, at.v, 1)

            run_visits(pe, pe_front, pe_both, pe_last)
            phase(pe, 2)
            pe.wait_ge(wup_in, 16)
            pe.sem_inc(ht_ready, 1)

            def pe_turn_outputs(g):
                pe.wait_ge(o_ready, g + 1)
                if not isinstance(g, int) or g > 0:
                    pe.wait_ge(x1_ready, g)
                for k in range(KH):
                    for i in range(2):
                        a = k * GT + i * P
                        last = pe.transpose(banks(0)[:, a:a + P], o_s[:, i, k * P:(k + 1) * P], ident[:])
                last.then_inc(ot_ps, 1)

            def pe_project(g):
                pe.wait_ge(ot_ready, g + 1)
                for i in range(2):
                    for n in range(2):
                        for k in range(KH):
                            last = pe.matmul(banks(2 * i + n), o_t[:, k, i * P:(i + 1) * P],
                                             wup_s[:, k, n * 512:(n + 1) * 512], start=(k == 0), stop=(k == KH - 1))
                last.then_inc(y_ps, 1)

            def pe_turn_h(g):
                pe.wait_ge(h_ready, g + 1)
                for k in range(KD):
                    for i in range(2):
                        a = k * GT + i * P
                        last = pe.transpose(banks(4, 4)[:, a:a + P], h_s[:, i, k * P:(k + 1) * P], ident[:])
                last.then_inc(ht_ps, 1)

            pe_turn_outputs(0)
            pe_project(0)
            pe_turn_outputs(1)
            with pe.Fori(0, NG - 2) as g:
                pe_project(g + 1)
                pe_turn_h(g)
                pe_turn_outputs(g + 2)
            pe_project(NG - 1)
            pe_turn_h(NG - 2)
            pe_turn_h(NG - 1)
            phase(pe, 3)

            def turned(g, a, w, m):
                for j in range(m):
                    for k in range(KD):
                        last = pe.matmul(banks(a, 2)[:, j * GT:(j + 1) * GT], w[:, k, j * P:(j + 1) * P],
                                         ht[:, k, bass.ds(g * GT, GT)], start=(k == 0), stop=(k == KD - 1))
                return last

            def pe_group(g, last_group=False):
                for i in range(2):
                    if i == 0:
                        pe.wait_ge(qt_ready, g + 2)
                    for j in range(HEADS):
                        last = pe.matmul(banks(6 * (1 - i), 2)[:, j * 2 * NK:(j + 1) * 2 * NK], qt[:, j, i * P:(i + 1) * P],
                                         keys_s[:, j, :, :].rearrange("p a n -> p (a n)"), start=True, stop=True)
                    last.then_inc(sim_ps, 1)
                pe.wait_ge(mlp_added, g + 1)
                turned(g, 2, wg_s, KI).then_inc(g_ps, 1)
                turned(g, 4, wu_s, KI).then_inc(u_ps, 1)
                if not last_group:
                    pe.wait_ge(sim_ready, 2 * g + 4)
                    turned(g + 1, 0, wq_s, HEADS).then_inc(q_ps, 1)
                pe.wait_ge(at_ready, g + 1)
                for i in range(2):
                    for n in range(2):
                        for k in range(KI):
                            last = pe.matmul(banks(2 + 2 * i + n), a_t[:, k, i * P:(i + 1) * P],
                                             wd_s[:, k, n * 512:(n + 1) * 512], start=(k == 0), stop=(k == KI - 1))
                last.then_inc(mlp_ps, 1)

            turned(0, 0, wq_s, HEADS).then_inc(q_ps, 1)
            with pe.Fori(0, NG - 1) as g:
                pe_group(g)
            pe_group(NG - 1, last_group=True)

            def pe_down(m, q, g):
                hg = ht[:, :, bass.ds(g * GT, GT)]
                if not isinstance(m, int) or m > 0:
                    pe.wait_ge(sd_act, m + 1)
                for j in range(EB):
                    for k in range(KD):
                        last = pe.matmul(banks(6, 2)[:, j * GT:(j + 1) * GT], dn_s[q][:, k, j * P:(j + 1) * P], hg[:, k, :],
                                         start=(k == 0), stop=(k == KD - 1))
                last.then_inc(d_ps, 1)

            def pe_turn_weights(m):
                pe.wait_ge(s_ready, m + 1)
                for b in range(EB):
                    for i in range(2):
                        a = b * GT + i * P
                        last = pe.transpose(banks(0, 2)[:, a:a + P], s_q[:, i, b, :], ident[:])
                last.then_inc(st_ps, 1)

            def pe_up(m_1, q):
                pe.wait_ge(v_ready, m_1 + 1)
                pe.wait_ge(yx_added, m_1)
                for i in range(2):
                    for n in range(2):
                        for b in range(EB):
                            last = pe.matmul(banks(2 + 2 * i + n), v_t[:, b, i * P:(i + 1) * P],
                                             up_s[q][:, b, n * 512:(n + 1) * 512], start=(b == 0), stop=(b == EB - 1))
                last.then_inc(yx_ps, 1)

            pe.wait_ge(dn_in[0], 16)
            pe.wait_ge(sim_ready, 2 * NG + 1)
            pe_down(0, 0, 0)
            phase(pe, 4)


            def pe_experts(m, q, g, before):
                first = isinstance(g, int)
                if first:
                    pe.wait_ge(dn_in[q], 16)
                pe_down(m, q, g)
                pe_up(m, q - 1 if first else q)
                pe_turn_weights(m)
                if first:
                    pe.wait_ge(up_in[q], 16)

            def pe_experts_start(m, q, g):
                pe_down(1, 0, 1)
                pe_turn_weights(0)
                pe.wait_ge(up_in[0], 16)
                pe_up(1, 0)
                pe_turn_weights(1)

            run_experts(pe, pe_experts_start, pe_experts, lambda before: pe_up(NG * QE, QE - 1), started=1)


def kernel(x, src, dst, L0_gnn_rms_w, L0_gnn_W_down, L0_gnn_Wl, L0_gnn_Wr, L0_gnn_att, L0_gnn_W_up, L0_ffn_Wq,
           L0_ffn_keys, L0_ffn_down_embed, L0_ffn_up_embed, L0_ffn_Wg, L0_ffn_Wu, L0_ffn_Wd):
    import numpy as np
    import concourse.bacc as bacc
    from concourse import mybir
    from concourse.bass_utils import run_bass_kernel_spmd

    chunk = 1024
    pad = -len(src) % chunk

    def by_partition(edges):
        return edges.reshape(-1, 8, 128).transpose(0, 2, 1).reshape(-1)

    src = np.pad(src, (0, pad))
    dst = np.pad(dst, (0, pad), constant_values=1 << 20)
    arrays = {
        "x": x,
        "src": by_partition(src),
        "dst": dst,
        "dst_cols": by_partition(dst),
        "rms_w": L0_gnn_rms_w.reshape(-1, 128).T,
        "w_down": L0_gnn_W_down,
        "w_l": L0_gnn_Wl,
        "w_r": L0_gnn_Wr,
        "att": L0_gnn_att,
        "w_up": L0_gnn_W_up,
        "wq_t": L0_ffn_Wq.T,
        "keys_t": L0_ffn_keys.transpose(3, 2, 0, 1),
        "down_t": L0_ffn_down_embed.T,
        "up": L0_ffn_up_embed,
        "wg_t": L0_ffn_Wg.T,
        "wu_t": L0_ffn_Wu.T,
        "wd_t": L0_ffn_Wd.T,
    }
    arrays = {f"in_{k}": np.ascontiguousarray(v) for k, v in arrays.items()}
    nc = bacc.Bacc("TRN2", target_bir_lowering=False, num_devices=1)
    args = [nc.dram_tensor(k, v.shape, mybir.dt.from_np(v.dtype), kind="ExternalInput").ap() for k, v in arrays.items()]
    out = nc.dram_tensor("out", x.shape, mybir.dt.float32, kind="ExternalOutput").ap()
    gnn_then_peer_ffn(nc, *args, out)
    r = run_bass_kernel_spmd(nc, [arrays], core_ids=[0])
    return r.results[0]["out"]
```
